# Optimizing a Trainium2 kernel written in Bass

```python
import numpy as np
import jax
import jax.numpy as jnp

def _softmax(x, axis=-1):
    return jax.nn.softmax(x, axis=axis)

def _gelu(x):
    return jax.nn.gelu(x, approximate=True)

def _silu(x):
    return jax.nn.silu(x)

def _sigmoid(x):
    return jax.nn.sigmoid(x)

def _layernorm(x, axis=-1, eps=1e-05):
    m = jnp.mean(x, axis=axis, keepdims=True)
    v = jnp.var(x, axis=axis, keepdims=True)
    return (x - m) / jnp.sqrt(v + eps)

def _scatter_add(tgt, idx, src, axis=0):
    return tgt.at[idx].add(src)

def _segment_sum(src, seg, n):
    return jax.ops.segment_sum(src, seg, n)
kernel_name = 'mk_vit_tower_d1_tok_img1024_r4_e19257'

def setup_inputs(seed: int=0):
    np.random.seed(seed)
    _w = jnp.asarray

    def _rec_inputs():
        import jax
        import jax.numpy as jnp
        _rk = jax.random.key(seed)
        x = -0.000222058 + 0.999998 * jax.random.normal(jax.random.fold_in(_rk, 1), (32, 3, 64, 64), jnp.float32)
        return x
    x = _rec_inputs()

    def _L0_tok_setup():
        import jax, jax.numpy as jnp
        import numpy as np
        IMG, PS, C, OUT = (64, 16, 3, 256)
        NP = IMG // PS
        IN_FEAT = C * PS * PS
        key = jax.random.key(seed)
        k1, k2, k3, k4 = jax.random.split(key, 4)
        x = jax.random.normal(k1, (128, C, IMG, IMG), dtype=jnp.float32)
        W = jax.random.normal(k2, (OUT, IN_FEAT), dtype=jnp.float32) / np.sqrt(IN_FEAT)
        b = jax.random.normal(k3, (OUT,), dtype=jnp.float32) * 0.01
        pos_emb = jax.random.normal(k4, (NP * NP, OUT), dtype=jnp.float32)
        return {'x': x, 'W': W, 'b': b, 'pos_emb': pos_emb}
    _L0_tok_all = _L0_tok_setup()
    _L0_tok_in = {k: v for k, v in _L0_tok_all.items() if k in ('W', 'b', 'pos_emb')}
    del _L0_tok_all

    def _L0_attn_setup():
        import jax, jax.numpy as jnp
        import numpy as np
        B, S, E, H = (2, 512, 256, 16)
        D = E // H
        NEG_INF = -1e+30

        def alibi_slopes(n_head):
            return jnp.asarray([2.0 ** (-8.0 * (i + 1) / n_head) for i in range(n_head)], dtype=jnp.float32)
        key = jax.random.key(seed)
        ks = jax.random.split(key, 5)
        scale = 0.02
        return {'x': jax.random.normal(ks[0], (B, S, E), dtype=jnp.float32), 'W_kqv': jax.random.normal(ks[1], (E, 3 * E), dtype=jnp.float32) * scale, 'b_kqv': jnp.zeros((3 * E,), dtype=jnp.float32), 'W_proj': jax.random.normal(ks[2], (E, E), dtype=jnp.float32) * scale, 'b_proj': jnp.zeros((E,), dtype=jnp.float32), 'slopes': alibi_slopes(H)}
    _L0_attn_all = _L0_attn_setup()
    _L0_attn_in = {k: v for k, v in _L0_attn_all.items() if k in ('W_kqv', 'b_kqv', 'W_proj', 'b_proj', 'slopes')}
    del _L0_attn_all

    def _L0_ffn_setup():
        import jax, jax.numpy as jnp
        import numpy as np

        def _bitlinear(x, w_latent):
            scale = jax.lax.stop_gradient(jnp.clip(jnp.mean(jnp.abs(w_latent), axis=1, keepdims=True), 1e-05, None))
            tern = jnp.clip(jnp.round(w_latent / scale), -1.0, 1.0)
            w = w_latent + jax.lax.stop_gradient(tern - w_latent)
            return x @ (w * scale).T
        key = jax.random.key(seed)
        ks = jax.random.split(key, 6)
        dim, hidden, rank = (256, 1024, 16)
        B, S = (4, 1024)
        x = jax.random.normal(ks[0], (B, S, dim), dtype=jnp.float32)
        w_fc = 0.02 * jax.random.normal(ks[1], (hidden, dim), dtype=jnp.float32)
        w_proj = 0.02 * jax.random.normal(ks[2], (dim, hidden), dtype=jnp.float32)
        u = 0.02 * jax.random.normal(ks[3], (hidden, rank), dtype=jnp.float32)
        v = 0.02 * jax.random.normal(ks[4], (rank, dim), dtype=jnp.float32)
        fast_b = jax.random.normal(ks[5], (rank, rank), dtype=jnp.float32)
        gate = jnp.float32(0.05)
        return {'x': x, 'fast_b': fast_b, 'w_fc': w_fc, 'w_proj': w_proj, 'u': u, 'v': v, 'gate': gate}
    _L0_ffn_all = _L0_ffn_setup()
    _L0_ffn_in = {k: v for k, v in _L0_ffn_all.items() if k in ('fast_b', 'w_fc', 'w_proj', 'u', 'v', 'gate')}
    del _L0_ffn_all
    return {'x': x, 'L0_tok_W': _L0_tok_in['W'], 'L0_tok_b': _L0_tok_in['b'], 'L0_tok_pos_emb': _L0_tok_in['pos_emb'], 'L0_attn_W_kqv': _L0_attn_in['W_kqv'], 'L0_attn_b_kqv': _L0_attn_in['b_kqv'], 'L0_attn_W_proj': _L0_attn_in['W_proj'], 'L0_attn_b_proj': _L0_attn_in['b_proj'], 'L0_attn_slopes': _L0_attn_in['slopes'], 'L0_ffn_fast_b': _L0_ffn_in['fast_b'], 'L0_ffn_w_fc': _L0_ffn_in['w_fc'], 'L0_ffn_w_proj': _L0_ffn_in['w_proj'], 'L0_ffn_u': _L0_ffn_in['u'], 'L0_ffn_v': _L0_ffn_in['v'], 'L0_ffn_gate': _L0_ffn_in['gate']}

def reference(x, L0_tok_W, L0_tok_b, L0_tok_pos_emb, L0_attn_W_kqv, L0_attn_b_kqv, L0_attn_W_proj, L0_attn_b_proj, L0_attn_slopes, L0_ffn_fast_b, L0_ffn_w_fc, L0_ffn_w_proj, L0_ffn_u, L0_ffn_v, L0_ffn_gate):
    import jax
    import jax.numpy as jnp

    def _L0_tok_ref(x, W, b, pos_emb):
        import jax, jax.numpy as jnp
        import numpy as np
        IMG, PS, C, OUT = (64, 16, 3, 256)
        NP = IMG // PS
        IN_FEAT = C * PS * PS
        B = x.shape[0]
        p = x.reshape(B, C, NP, PS, NP, PS).transpose(0, 1, 2, 4, 3, 5)
        p = p.transpose(0, 2, 3, 1, 4, 5)
        p = p.reshape(B, NP * NP, IN_FEAT)
        out = jnp.einsum('bnf,of->bno', p, W) + b + pos_emb
        return out

    def _L0_attn_ref(x, W_kqv, b_kqv, W_proj, b_proj, slopes):
        import jax, jax.numpy as jnp
        import numpy as np
        B, S, E, H = (2, 512, 256, 16)
        D = E // H
        NEG_INF = -1e+30

        def alibi_slopes(n_head):
            return jnp.asarray([2.0 ** (-8.0 * (i + 1) / n_head) for i in range(n_head)], dtype=jnp.float32)
        b, s, e = x.shape
        kqv = x @ W_kqv + b_kqv
        k, q, v = jnp.split(kqv, 3, axis=-1)
        k = k.reshape(b, s, H, D)
        q = q.reshape(b, s, H, D)
        v = v.reshape(b, s, H, D)
        attn = jnp.einsum('bqhd,bkhd->bhqk', q, k) * (1.0 / jnp.sqrt(jnp.float32(D)))
        i = jnp.arange(s)[:, None]
        j = jnp.arange(s)[None, :]
        rel = (j - i).astype(jnp.float32)
        bias = slopes[:, None, None] * jnp.tril(rel)
        bias = jnp.where(j > i, NEG_INF, bias)
        attn = jax.nn.softmax(attn + bias[None], axis=-1)
        y = jnp.einsum('bhqk,bkhd->bqhd', attn, v).reshape(b, s, e)
        return y @ W_proj + b_proj

    def _L0_ffn_ref(x, fast_b, w_fc, w_proj, u, v, gate):
        import jax, jax.numpy as jnp
        import numpy as np

        def _bitlinear(x, w_latent):
            scale = jax.lax.stop_gradient(jnp.clip(jnp.mean(jnp.abs(w_latent), axis=1, keepdims=True), 1e-05, None))
            tern = jnp.clip(jnp.round(w_latent / scale), -1.0, 1.0)
            w = w_latent + jax.lax.stop_gradient(tern - w_latent)
            return x @ (w * scale).T
        h = _bitlinear(x, w_fc) + gate * (x @ v.T @ fast_b.T @ u.T)
        r = jnp.maximum(h, 0.0)
        return _bitlinear(r * r, w_proj)
    h = _L0_tok_ref(x, L0_tok_W, L0_tok_b, L0_tok_pos_emb)
    h = h + _L0_attn_ref(_layernorm(h, axis=-1), L0_attn_W_kqv, L0_attn_b_kqv, L0_attn_W_proj, L0_attn_b_proj, L0_attn_slopes)
    h = h + _L0_ffn_ref(_layernorm(h, axis=-1), L0_ffn_fast_b, L0_ffn_w_fc, L0_ffn_w_proj, L0_ffn_u, L0_ffn_v, L0_ffn_gate)
    return h

_drawn_inputs = setup_inputs


def setup_inputs(seed=0):
    import zlib

    import numpy as np

    out = dict(_drawn_inputs(seed))
    spreads = {'L0_attn_b_kqv': (0.0, 0.389), 'L0_attn_b_proj': (0.0, 0.1)}
    factors = {'L0_tok_b': 7.745,
     'L0_attn_slopes': 4.606,
     'L0_ffn_fast_b': 8.0,
     'L0_ffn_w_fc': 3.733,
     'L0_ffn_w_proj': 3.43,
     'L0_ffn_u': 8.0,
     'L0_ffn_v': 8.0}
    for name, (base, spread) in spreads.items():
        noise = np.random.default_rng([zlib.crc32(name.encode()), seed]).standard_normal(out[name].shape)
        drawn = base * np.exp(spread * noise) if base else spread * noise
        out[name] = jnp.asarray(drawn.astype(out[name].dtype))
    for name, factor in factors.items():
        out[name] = (out[name] * factor).astype(out[name].dtype)
    return out
```

```python
from contextlib import ExitStack

import numpy as np

import concourse.bass as bass
from concourse import mybir

F32 = mybir.dt.float32
F32R = mybir.dt.float32r
BF16 = mybir.dt.bfloat16
ALU = mybir.AluOpType
ACT = mybir.ActivationFunctionType
AX = mybir.AxisListType

P = 128
IMAGES, CH, IMG, PATCH = 32, 3, 64, 16
SIDE = IMG // PATCH
S = SIDE * SIDE
TOK = IMAGES * S
FEAT = CH * PATCH * PATCH
E = 256
H, D = 16, 16
HID, RANK = 1024, 16
KF, KE, KH = FEAT // P, E // P, HID // P
HALVES = 2
HT = TOK // HALVES
BH = HT // P
BLOCKS = TOK // P
IPB = P // S
HPG = P // D
GRP = H // HPG
IPH = IMAGES // HALVES
NEG_INF = -1e30
EPS = 1e-5
SPREAD_DVE = 5

C_ID, C_MASK, C_REL, C_NEG = 0, P, P + 8, P + 8 + S
C_END = C_NEG + S
R_TOKB, R_VB, R_PB, R_GATE = 0, E, 2 * E, 3 * E
R_END = 3 * E + 1


def build_program(nc, x_t, wtok_t, consts, rows, pos, w_kqv, qk_bias, slopes, w_proj, w_fc, w_mlp,
                  u_nat, v_t, fb_t, out_t):
    with ExitStack() as ctx:
        def sb(name, shape, dt=F32):
            return ctx.enter_context(nc.sbuf_tensor(name, shape, dt))

        def sem(name):
            return ctx.enter_context(nc.semaphore(name))

        bank = [ctx.enter_context(nc.psum_tensor(f"bank{i}", [P, 512], F32)) for i in range(8)]

        x_sb = sb("x_sb", [P, KF, TOK])
        wtok_sb = sb("wtok_sb", [P, KF, E])
        const_sb = sb("const_sb", [P, C_END])
        rows_sb = sb("rows_sb", [P, R_END])
        pos_sb = sb("pos_sb", [P, E])
        kqv_sb = sb("kqv_sb", [P, KE, 3 * E])
        qkb_sb = sb("qkb_sb", [P, 2 * GRP])
        slope_sb = sb("slope_sb", [P, GRP])
        proj_sb = sb("proj_sb", [P, KE, E])
        fc_sb = sb("fc_sb", [P, KH, E])
        mlp_sb = sb("mlp_sb", [P, KE, HID])
        u_sb = sb("u_sb", [P, KH, RANK])
        v_sb = sb("v_sb", [P, KE, RANK])
        fb_sb = sb("fb_sb", [2 * RANK, 4 * RANK])

        ident = const_sb[:, C_ID:C_ID + P]
        mask = const_sb[:, C_MASK:C_MASK + 8]
        rel = const_sb[:, C_REL:C_REL + S]
        neg = const_sb[:, C_NEG:C_NEG + S]

        ident_bf = sb("ident_bf", [P, P], BF16)
        posb = sb("posb", [P, E])
        alibi = sb("alibi", [P, GRP, S])
        kqv_hi = sb("kqv_hi", [P, KE, 3 * E], F32R)
        kqv_lo = sb("kqv_lo", [P, KE, 3 * E], F32R)
        proj_hi = sb("proj_hi", [P, KE, E], F32R)
        proj_lo = sb("proj_lo", [P, KE, E], F32R)
        v_parts = sb("v_parts", [P, KE, 2, RANK], F32R)
        fc_sum = sb("fc_sum", [P, KH])
        mlp_sum = sb("mlp_sum", [P, KE])
        fc_scale = sb("fc_scale", [P, 4, KH])
        mlp_scale = sb("mlp_scale", [P, 3, KE])
        fc_below = sb("fc_below", [P, KH, E], BF16)
        fc_tern = sb("fc_tern", [P, KH, E], BF16)
        mlp_below = sb("mlp_below", [P, KE, HID], BF16)
        mlp_tern = sb("mlp_tern", [P, KE, HID], BF16)
        fc_t = sb("fc_t", [P, KE, HID], F32R)
        mlp_t = sb("mlp_t", [P, KH, E], F32R)
        u_scaled = sb("u_scaled", [P, KH, RANK])
        u_parts = sb("u_parts", [P, KH, 4, RANK], F32R)
        u_t = sb("u_t", [4 * RANK, HID], F32R)
        eps_sb = sb("eps_sb", [P, 1])

        h1 = sb("h1", [P, BLOCKS, E])
        h1b = sb("h1b", [P, BLOCKS, E])
        h2 = sb("h2", [P, BLOCKS, E])
        bn6 = sb("bn6", [P, 2, BLOCKS, 6])
        mv = sb("mv", [P, 2, BLOCKS, 2])
        std = sb("std", [P, 2, BLOCKS])
        rstd = sb("rstd", [P, 2, BLOCKS])
        z = sb("z", [P, BLOCKS, E])
        zt_hi = [sb(f"zt_hi{f}", [P, KE, HT], F32R) for f in range(HALVES)]
        zt_lo = [sb(f"zt_lo{f}", [P, KE, HT], F32R) for f in range(HALVES)]
        q_t = sb("q_t", [P, HALVES, GRP, HT])
        k_t = sb("k_t", [P, HALVES, GRP, HT])
        v_tok = sb("v_tok", [P, HALVES, BH, E])
        q_spread = sb("q_spread", [P, HALVES, GRP * IPH, HPG, S])
        p_spread = q_spread
        abs_junk = q_spread[:, 0, 0:HPG, :, :].rearrange("p n a s -> p (n a s)")
        smax = sb("smax", [P, HALVES, GRP * IPH])
        ssum = sb("ssum", [P, HALVES, GRP * IPH])
        srec = sb("srec", [P, HALVES, GRP * IPH])

        def reuse(base, lot):
            flat = base[:, :, :].rearrange("p k n -> p (k n)")
            return flat[:, lot * HALVES * 2 * HT:(lot + 1) * HALVES * 2 * HT]

        score = reuse(x_sb, 0).rearrange("p (f g i s) -> p f g i s", f=HALVES, g=GRP, s=S)
        shifted = reuse(x_sb, 1).rearrange("p (f n s) -> p f n s", f=HALVES, s=S)
        expd = reuse(x_sb, 2).rearrange("p (f n s) -> p f n s", f=HALVES, s=S)
        p_t = reuse(fc_sb, 0).rearrange("p (f n s) -> p f n s", f=HALVES, s=S)
        y_tok = reuse(fc_sb, 1).rearrange("p (f b e) -> p f b e", f=HALVES, b=BH)
        prob = reuse(mlp_sb, 0).rearrange("p (f g n) -> p f g n", f=HALVES, g=GRP)
        h2_t = reuse(mlp_sb, 1).rearrange("p (f k t) -> p f k t", f=HALVES, k=KE)
        yt_hi = [sb(f"yt_hi{f}", [P, GRP, HT], F32R) for f in range(HALVES)]
        yt_lo = [sb(f"yt_lo{f}", [P, GRP, HT], F32R) for f in range(HALVES)]
        z2t_hi = [sb(f"z2t_hi{f}", [P, KE, HT], F32R) for f in range(HALVES)]
        z2t_lo = [sb(f"z2t_lo{f}", [P, KE, HT], F32R) for f in range(HALVES)]
        low_a = sb("low_a", [2 * RANK, HALVES, HT])
        low_t = sb("low_t", [4 * RANK, HALVES, HT], F32R)
        RING = 3
        relu = wtok_sb[:, :, :].rearrange("p (r a) t -> p r a t", a=2)
        sq = kqv_sb[:, :, :].rearrange("p k n -> p (k n)").rearrange("p (r a t) -> p r a t", r=RING, a=2)
        sq_hi = sb("sq_hi", [P, RING, 2, HT], F32R)
        sq_lo = sb("sq_lo", [P, RING, 2, HT], F32R)
        out_sb = q_t

        tok_ps = [bank[b][:, 0:E] for b in range(BLOCKS)]
        fct_ps = [bank[6 + k][:, :].bitcast(BF16) for k in range(KE)]
        ut_ps = [bank[6 + i][0:4 * RANK, :] for i in range(2)]
        zt_ps = [bank[4 + f] for f in range(HALVES)]
        k_ps = [bank[0 + f] for f in range(HALVES)]
        q_ps = [bank[2 + f] for f in range(HALVES)]
        v_ps = [bank[6 + f] for f in range(HALVES)]
        s_ps = [bank[4 + f] for f in range(HALVES)]
        mlpt_ps = [bank[6 + i][:, :].bitcast(BF16) for i in range(2)]
        pt_ps = [bank[0 + f] for f in range(HALVES)]
        y_ps = [bank[2 + f] for f in range(HALVES)]
        yt_ps = [bank[6 + f] for f in range(HALVES)]
        o_ps = [bank[4 + f] for f in range(HALVES)]
        z2t_ps = [bank[0 + f] for f in range(HALVES)]
        h2t_ps = [bank[2 + f] for f in range(HALVES)]
        low_ps = [bank[6 + f] for f in range(HALVES)]
        FCB = [bank[4], bank[5], bank[0], bank[1]]
        mlp_ps = [bank[2 + f] for f in range(HALVES)]

        tok_in = [sem(f"tok_in{k}") for k in range(KF)]
        const_in = sem("const_in")
        rows_in = sem("rows_in")
        kqv_in = sem("kqv_in")
        small_in = sem("small_in")
        proj_in = sem("proj_in")
        fc_in = sem("fc_in")
        mlp_in = sem("mlp_in")
        out_done = sem("out_done")
        eps_set = sem("eps_set")
        identbf_done = sem("identbf_done")
        posb_done = sem("posb_done")
        alibi_done = sem("alibi_done")
        kqv_split = sem("kqv_split")
        proj_split = sem("proj_split")
        v_split = sem("v_split")
        fc_summed = sem("fc_summed")
        mlp_summed = sem("mlp_summed")
        fc_scaled = sem("fc_scaled")
        mlp_scaled = sem("mlp_scaled")
        fc_cmp = sem("fc_cmp")
        fc_ternary = sem("fc_ternary")
        mlp_cmp = sem("mlp_cmp")
        mlp_ternary = sem("mlp_ternary")
        fct_turned = sem("fct_turned")
        fct_ready = sem("fct_ready")
        mlpt_turned = sem("mlpt_turned")
        mlpt_ready = sem("mlpt_ready")
        u_step = sem("u_step")
        ut_turned = sem("ut_turned")
        ut_ready = sem("ut_ready")
        tok_done = sem("tok_done")
        h1_ready = sem("h1_ready")
        h1b_ready = sem("h1b_ready")
        bn1 = sem("bn1")
        var1 = sem("var1")
        std1 = sem("std1")
        rstd1 = sem("rstd1")
        z1_ready = sem("z1_ready")
        zt_turned = sem("zt_turned")
        zt_hi_ready = sem("zt_hi_ready")
        zt_lo_ready = sem("zt_lo_ready")
        q_done = sem("q_done")
        k_done = sem("k_done")
        v_done = sem("v_done")
        q_ready = sem("q_ready")
        k_ready = sem("k_ready")
        v_ready = sem("v_ready")
        q_spread_dve = sem("q_spread_dve")
        q_spread_act = sem("q_spread_act")
        s_done = sem("s_done")
        score_ready = sem("score_ready")
        max_ready = sem("max_ready")
        shift_ready = sem("shift_ready")
        exp_ready = sem("exp_ready")
        sum_ready = sem("sum_ready")
        rec_ready = sem("rec_ready")
        prob_ready = sem("prob_ready")
        pt_turned = sem("pt_turned")
        pt_ready = sem("pt_ready")
        p_spread_dve = sem("p_spread_dve")
        p_spread_act = sem("p_spread_act")
        y_done = sem("y_done")
        y_ready = sem("y_ready")
        yt_turned = sem("yt_turned")
        yt_hi_ready = sem("yt_hi_ready")
        yt_lo_ready = sem("yt_lo_ready")
        o_done = sem("o_done")
        h2_ready = sem("h2_ready")
        bn2 = sem("bn2")
        var2 = sem("var2")
        std2 = sem("std2")
        rstd2 = sem("rstd2")
        z2_ready = sem("z2_ready")
        z2t_turned = sem("z2t_turned")
        h2t_turned = sem("h2t_turned")
        h2t_ready = sem("h2t_ready")
        z2t_hi_ready = sem("z2t_hi_ready")
        z2t_lo_ready = sem("z2t_lo_ready")
        low_a_done = sem("low_a_done")
        low_a_ready = sem("low_a_ready")
        low_c_done = sem("low_c_done")
        low_hi_ready = sem("low_hi_ready")
        low_ready = sem("low_ready")
        fc_done = sem("fc_done")
        relu_ready = sem("relu_ready")
        sq_ready = sem("sq_ready")
        sq_hi_ready = sem("sq_hi_ready")
        sq_lo_ready = sem("sq_lo_ready")
        mlp_step = sem("mlp_step")
        mlp_done = sem("mlp_done")
        out_ready = sem("out_ready")

        block = ctx.enter_context(nc.Block())
        SMALL_LOADS = 6
        PAIRS = KH // 2

        @block.sync
        def _(sp):
            for k in range(KF):
                sp.dma_start(x_sb[:, k, :], x_t[k * P:(k + 1) * P, :]).then_inc(tok_in[k], 16)
                sp.dma_start(wtok_sb[:, k, :], wtok_t[k * P:(k + 1) * P, :]).then_inc(tok_in[k], 16)
            sp.dma_start(kqv_sb[:, :, :], w_kqv.rearrange("(k p) n -> p k n", p=P)).then_inc(kqv_in, 16)
            sp.dma_start(mlp_sb[:, :, :], w_mlp.rearrange("(k p) n -> p k n", p=P)).then_inc(mlp_in, 16)
            sp.dma_start(proj_sb[:, :, :], w_proj.rearrange("(k p) n -> p k n", p=P)).then_inc(proj_in, 16)
            for f in range(HALVES):
                for m in range(KE):
                    sp.wait_ge(out_ready, f * KE + m + 1)
                    sp.dma_start(out_t[m * P:(m + 1) * P, f * HT:(f + 1) * HT],
                                 out_sb[:, f, m, :]).then_inc(out_done, 16)
            sp.wait_ge(out_done, 16 * HALVES * KE)

        @block.tensor
        def _(pe):
            def split_product(out, pairs, start=True):
                for i, (lhs, rhs) in enumerate(pairs):
                    mm = pe.matmul(out, lhs, rhs, start=start and i == 0, stop=i == len(pairs) - 1)
                return mm

            def embed(k, b):
                return pe.matmul(tok_ps[b], x_sb[:, k, b * P:(b + 1) * P], wtok_sb[:, k, :],
                                 start=k == 0, stop=k == KF - 1)

            for k in range(KF // 2):
                pe.wait_ge(tok_in[k], 32)
                for b in range(BLOCKS):
                    embed(k, b)
            for b in range(BLOCKS):
                for k in range(KF // 2, KF):
                    if b == 0:
                        pe.wait_ge(tok_in[k], 32)
                    mm = embed(k, b)
                mm.then_inc(tok_done, 1)

            pe.wait_ge(identbf_done, 1)
            pe.wait_ge(fc_ternary, KH)
            for k in range(KE):
                for m in range(KH):
                    mm = pe.transpose(fct_ps[k][:, m * P:(m + 1) * P],
                                      fc_tern[:, m, k * P:(k + 1) * P], ident_bf[:, :])
                mm.then_inc(fct_turned, 1)

            def turn_z(f, src, dst, ready, signal):
                for b in range(BH):
                    pe.wait_ge(ready, f * BH + b + 1)
                    for k in range(KE):
                        mm = pe.transpose(dst[:, k * HT + b * P:k * HT + (b + 1) * P],
                                          src(f * BH + b)[:, k * P:(k + 1) * P], ident)
                mm.then_inc(signal, 1)

            def qkv(f):
                pe.wait_ge(kqv_split, 2)
                pe.wait_ge(zt_hi_ready, f + 1)
                pe.wait_ge(zt_lo_ready, f + 1)
                for which, ps, signal in ((1, q_ps[f], q_done), (0, k_ps[f], k_done)):
                    pe.wait_ge(h1_ready, (2 * which + f) + 1)
                    for g in range(GRP):
                        c = which * E + g * P
                        pairs = []
                        for k in range(KE):
                            hi, lo = kqv_hi[:, k, c:c + P], kqv_lo[:, k, c:c + P]
                            pairs += [(hi, zt_hi[f][:, k, :]), (hi, zt_lo[f][:, k, :]),
                                      (lo, zt_hi[f][:, k, :])]
                        mm = split_product(ps[:, g * HT:(g + 1) * HT], pairs)
                    mm.then_inc(signal, 1)
                pe.wait_ge(ut_ready, f + 1)
                for b in range(BH):
                    pairs = []
                    for k in range(KE):
                        zh, zl = (t[f][:, k, b * P:(b + 1) * P] for t in (zt_hi, zt_lo))
                        wh, wl = (t[:, k, 2 * E:3 * E] for t in (kqv_hi, kqv_lo))
                        pairs += [(zh, wh), (zh, wl), (zl, wh)]
                    mm = split_product(v_ps[f][:, b * E:(b + 1) * E], pairs)
                mm.then_inc(v_done, 1)

            def scores(f):
                pe.wait_ge(k_ready, GRP * (f + 1))
                pe.wait_ge(q_spread_dve, f + 1)
                pe.wait_ge(q_spread_act, f + 1)
                for g in range(GRP):
                    for i in range(IPH):
                        gi = g * IPH + i
                        mm = pe.matmul(s_ps[f][:, gi * S:(gi + 1) * S], q_spread[:, f, gi, :, :],
                                       k_t[:, f, g, i * S:(i + 1) * S], start=True, stop=True)
                mm.then_inc(s_done, 1)

            def turn_probs(f):
                pe.wait_ge(prob_ready, f + 1)
                for b in range(BH):
                    for g in range(GRP):
                        c = (b * GRP + g) * P
                        mm = pe.transpose(pt_ps[f][:, c:c + P], prob[:, f, g, b * P:(b + 1) * P], ident)
                mm.then_inc(pt_turned, 1)

            def values(f):
                pe.wait_ge(v_ready, f + 1)
                pe.wait_ge(p_spread_dve, f + 1)
                pe.wait_ge(p_spread_act, f + 1)
                for b in range(BH):
                    for h in range(H):
                        c = b * E + h * D
                        mm = pe.matmul(y_ps[f][:, c:c + D], p_spread[:, f, b * H + h, :, :],
                                       v_tok[:, f, b, h * D:(h + 1) * D], start=True, stop=True)
                mm.then_inc(y_done, 1)

            def turn_y(f):
                pe.wait_ge(y_ready, f + 1)
                pe.wait_ge(mlpt_ready, f + 1)
                for b in range(BH):
                    for g in range(GRP):
                        c = g * HT + b * P
                        mm = pe.transpose(yt_ps[f][:, c:c + P], y_tok[:, f, b, g * P:(g + 1) * P], ident)
                mm.then_inc(yt_turned, 1)

            def project(f):
                pe.wait_ge(proj_split, 2)
                pe.wait_ge(yt_hi_ready, f + 1)
                pe.wait_ge(yt_lo_ready, f + 1)
                for b in range(BH):
                    pairs = []
                    for g in range(GRP):
                        yh, yl = (t[f][:, g, b * P:(b + 1) * P] for t in (yt_hi, yt_lo))
                        pairs += [(yh, proj_hi[:, g, :]), (yh, proj_lo[:, g, :]), (yl, proj_hi[:, g, :])]
                    mm = split_product(o_ps[f][:, b * E:(b + 1) * E], pairs)
                mm.then_inc(o_done, 1)

            def low_rank_a(f):
                pe.wait_ge(v_split, 2)
                pe.wait_ge(z2t_hi_ready, f + 1)
                pe.wait_ge(z2t_lo_ready, f + 1)
                pairs = []
                for k in range(KE):
                    vp = v_parts[:, k, :, :]
                    pairs += [(vp, z2t_hi[f][:, k, :]), (vp, z2t_lo[f][:, k, :])]
                split_product(low_ps[f][0:2 * RANK, 0:HT], pairs).then_inc(low_a_done, 1)

            def low_rank_c(f):
                pe.wait_ge(low_a_ready, f + 1)
                pe.wait_ge(small_in, 16 * SMALL_LOADS)
                pe.matmul(low_ps[f][0:4 * RANK, HT:2 * HT], fb_sb[:, :], low_a[:, f, :],
                          start=True, stop=True).then_inc(low_c_done, 1)

            def hidden(f, j):
                n = f * PAIRS + j
                if n >= len(FCB):
                    pe.wait_ge(relu_ready, 2 * (n - len(FCB) + 1))
                ps = FCB[n % len(FCB)]
                for a in range(2):
                    m = 2 * j + a
                    out = ps[:, a * HT:(a + 1) * HT]
                    pairs = []
                    for k in range(KE):
                        w = fc_t[:, k, m * P:(m + 1) * P]
                        pairs += [(w, z2t_hi[f][:, k, :]), (w, z2t_lo[f][:, k, :])]
                    for i, (lhs, rhs) in enumerate(pairs):
                        pe.matmul(out, lhs, rhs, start=i == 0, stop=False)
                    if j == 0 and a == 0:
                        pe.wait_ge(low_ready, f + 1)
                    mm = pe.matmul(out, u_t[:, m * P:(m + 1) * P], low_t[:, f, :], start=False, stop=True)
                mm.then_inc(fc_done, 1)

            def mlp_out(f, j):
                n = f * PAIRS + j
                pe.wait_ge(sq_hi_ready, n + 1)
                pe.wait_ge(sq_lo_ready, n + 1)
                for a in range(2):
                    for m in range(KE):
                        w = mlp_t[:, 2 * j + a, m * P:(m + 1) * P]
                        for i, part in enumerate((sq_hi, sq_lo)):
                            first = j == 0 and a == 0 and i == 0
                            mm = pe.matmul(mlp_ps[f][:, m * HT:(m + 1) * HT], w,
                                           part[:, n % RING, a, :], start=first and m == 0,
                                           stop=j == PAIRS - 1 and a == 1 and i == 1,
                                           skip_group_check=True)
                mm.then_inc(mlp_step, 1)

            turn_z(0, lambda b: z[:, b, :], zt_ps[0], z1_ready, zt_turned)
            for i in range(2):
                pe.wait_ge(u_step, 6)
                pe.wait_ge(fct_ready, i + 1)
                for m in range(4):
                    mm = pe.transpose(ut_ps[i][:, m * P:(m + 1) * P],
                                      u_parts[:, 4 * i + m, :, :].bitcast(F32), ident)
                mm.then_inc(ut_turned, 1)
            turn_z(1, lambda b: z[:, b, :], zt_ps[1], z1_ready, zt_turned)
            qkv(0)
            qkv(1)
            scores(0)
            scores(1)
            for i in range(2):
                pe.wait_ge(v_ready, i + 1)
                pe.wait_ge(mlp_ternary, KE)
                for m in range(4):
                    for o in range(KE):
                        c = (m * KE + o) * P
                        mm = pe.transpose(mlpt_ps[i][:, c:c + P],
                                          mlp_tern[:, o, (4 * i + m) * P:(4 * i + m + 1) * P],
                                          ident_bf[:, :])
                mm.then_inc(mlpt_turned, 1)
            turn_probs(0)
            values(0)
            turn_probs(1)
            turn_y(0)
            values(1)
            project(0)
            turn_y(1)
            project(1)

            def second_norm_turns(f):
                turn_z(f, lambda b: z[:, b, :], z2t_ps[f], z2_ready, z2t_turned)
                turn_z(f, lambda b: h2[:, b, :], h2t_ps[f], h2_ready, h2t_turned)

            second_norm_turns(0)
            low_rank_a(0)
            low_rank_c(0)
            pe.wait_ge(h2_ready, BH)
            pe.wait_ge(fct_ready, KE)
            pe.wait_ge(ut_ready, 2)
            second_norm_turns(1)
            hidden(0, 0)
            pe.wait_ge(h2_ready, BLOCKS)
            hidden(0, 1)
            low_rank_a(1)
            low_rank_c(1)
            hidden(0, 2)
            pe.wait_ge(h2t_ready, 1)
            mlp_out(0, 0)
            pe.wait_ge(z2t_hi_ready, 2)
            pe.wait_ge(z2t_lo_ready, 2)
            hidden(0, 3)
            mlp_out(0, 1)
            hidden(1, 0)
            mlp_out(0, 2)
            hidden(1, 1)
            mlp_out(0, 3)
            hidden(1, 2)
            pe.wait_ge(h2t_ready, 2)
            mlp_out(1, 0)
            hidden(1, 3)
            mlp_out(1, 1)
            mlp_out(1, 2)
            mlp_out(1, 3)

        @block.scalar
        def _(act):
            act.dma_start(const_sb[:, :], consts).then_inc(const_in, 16)
            act.dma_start(fc_sb[:, :, :], w_fc.rearrange("(m p) e -> p m e", p=P)).then_inc(fc_in, 16)
            act.dma_start(pos_sb[:, :], pos).then_inc(rows_in, 16)
            act.dma_start(rows_sb[:, :], rows.broadcast_to([P, R_END])).then_inc(rows_in, 16)
            act.dma_start(qkb_sb[:, :], qk_bias).then_inc(small_in, 16)
            act.dma_start(slope_sb[:, :], slopes).then_inc(small_in, 16)
            act.dma_start(u_sb[:, :, :], u_nat.rearrange("(m p) r -> p m r", p=P)).then_inc(small_in, 16)
            act.dma_start(v_sb[:, :, :], v_t.rearrange("(k p) r -> p k r", p=P)).then_inc(small_in, 16)
            for i in range(2):
                act.dma_start(fb_sb[i * RANK:(i + 1) * RANK, :].rearrange("p (a r) -> p a r", a=4),
                              fb_t.rearrange("p (o r) -> p o r", o=1).broadcast_to([RANK, 4, RANK])
                              ).then_inc(small_in, 16)

            act.wait_ge(fc_in, 16)
            for m in range(KH):
                nc.scalar.activation(abs_junk[:, 0:E], fc_sb[:, m, :], ACT.Abs,
                                     accum_out=fc_sum[:, m:m + 1]).then_inc(fc_summed, 1)
                act.wait_ge(fc_summed, m + 1)

            def norm_std(which, var_ready, std_ready, f):
                act.wait_ge(var_ready, BH * (f + 1))
                nc.scalar.activation(std[:, which, f * BH:(f + 1) * BH],
                                     mv[:, which, f * BH:(f + 1) * BH, 1], ACT.Sqrt,
                                     bias=eps_sb[:, 0:1]).then_inc(std_ready, 1)

            def copy_out(dst, src, turned, count, ready):
                act.wait_ge(turned, count)
                nc.scalar.activation(dst, src, ACT.Copy).then_inc(ready, 1)

            act.wait_ge(mlp_in, 16)
            for o in range(KE):
                nc.scalar.activation(abs_junk[:, :], mlp_sb[:, o, :], ACT.Abs,
                                     accum_out=mlp_sum[:, o:o + 1]).then_inc(mlp_summed, 1)
                act.wait_ge(mlp_summed, o + 1)
            act.wait_ge(eps_set, 1)
            norm_std(0, var1, std1, 0)
            for k in range(KE):
                copy_out(fc_t[:, k, :], fct_ps[k], fct_turned, k + 1, fct_ready)
            norm_std(0, var1, std1, 1)
            copy_out(zt_hi[0][:, :, :], zt_ps[0][:, :], zt_turned, 1, zt_hi_ready)
            for i in range(2):
                copy_out(u_t[:, i * HT * 2:(i + 1) * HT * 2], ut_ps[i], ut_turned, i + 1, ut_ready)
            copy_out(zt_hi[1][:, :, :], zt_ps[1][:, :], zt_turned, 2, zt_hi_ready)

            def bias_out(f, which, ps, done, dst, ready):
                act.wait_ge(done, f + 1)
                for g in range(GRP):
                    c = which * GRP + g
                    nc.scalar.activation(dst[:, f, g, :], ps[f][:, g * HT:(g + 1) * HT], ACT.Identity,
                                         bias=qkb_sb[:, c:c + 1]).then_inc(ready, 1)

            def spread(f, dst, src, ready, count, signal):
                act.wait_ge(ready, count)
                for a in range(SPREAD_DVE, 8):
                    last = nc.scalar.activation(dst[:, f, :, a, :], src, ACT.Copy, scale=mask[:, a:a + 1])
                last.then_inc(signal, 1)

            def q_strips(f):
                src = q_t[:, f, :, :].rearrange("p g (i s) -> p (g i) s", s=S)
                spread(f, q_spread, src, q_ready, GRP * (f + 1), q_spread_act)

            def p_strips(f):
                spread(f, p_spread, p_t[:, f, :, :], pt_ready, f + 1, p_spread_act)

            act.wait_ge(small_in, 16 * SMALL_LOADS)
            act.wait_ge(const_in, 16)
            for f in range(HALVES):
                bias_out(f, 1, q_ps, q_done, q_t, q_ready)
                q_strips(f)
                bias_out(f, 0, k_ps, k_done, k_t, k_ready)

            def exponentials(f):
                act.wait_ge(shift_ready, f + 1)
                nc.scalar.activation(expd[:, f, :, :], shifted[:, f, :, :], ACT.Exp).then_inc(exp_ready, 1)

            exponentials(0)
            copy_out(p_t[:, 0, :, :], pt_ps[0][:, :], pt_turned, 1, pt_ready)
            p_strips(0)
            exponentials(1)
            for i in range(2):
                copy_out(mlp_t[:, 4 * i:4 * i + 4, :], mlpt_ps[i], mlpt_turned, i + 1, mlpt_ready)
            copy_out(p_t[:, 1, :, :], pt_ps[1][:, :], pt_turned, 2, pt_ready)
            p_strips(1)
            for f in range(HALVES):
                copy_out(y_tok[:, f, :, :], y_ps[f][:, :], y_done, f + 1, y_ready)
                copy_out(yt_hi[f][:, :, :], yt_ps[f][:, :], yt_turned, f + 1, yt_hi_ready)
            for f in range(HALVES):
                norm_std(1, var2, std2, f)
                copy_out(z2t_hi[f][:, :, :], z2t_ps[f][:, :], z2t_turned, f + 1, z2t_hi_ready)
                copy_out(h2_t[:, f, :, :], h2t_ps[f][:, :], h2t_turned, f + 1, h2t_ready)
                act.wait_ge(low_c_done, f + 1)
                nc.scalar.activation(low_t[:, f, :], low_ps[f][0:4 * RANK, HT:2 * HT],
                                     ACT.Copy).then_inc(low_hi_ready, 1)

            for n in range(HALVES * PAIRS):
                f, j = divmod(n, PAIRS)
                if n >= RING:
                    act.wait_ge(sq_ready, n - RING + 1)
                act.wait_ge(fc_done, n + 1)
                for a in range(2):
                    m = 2 * j + a
                    nc.scalar.activation(relu[:, n % RING, a, :], FCB[n % len(FCB)][:, a * HT:(a + 1) * HT],
                                         ACT.Relu, scale=fc_scale[:, 0, m:m + 1]).then_inc(relu_ready, 1)
                if n >= RING:
                    act.wait_ge(mlp_step, n - RING + 1)
                act.wait_ge(relu_ready, 2 * n + 2)
                nc.scalar.activation(sq_hi[:, n % RING, :, :], relu[:, n % RING, :, :],
                                     ACT.Square).then_inc(sq_hi_ready, 1)

        @block.vector
        def _(dve):
            dve.memset(eps_sb[:, :], EPS).then_inc(eps_set, 1)
            dve.wait_ge(const_in, 16)
            dve.tensor_copy(ident_bf[:, :], ident).then_inc(identbf_done, 1)

            def scales(sums, scale, n, length, summed, scaled):
                dve.wait_ge(summed, n)
                dve.tensor_scalar(scale[:, 0, :], sums[:, :], 1.0 / length, EPS, ALU.mult,
                                  ALU.max).then_inc(scaled, 1)
                dve.wait_ge(scaled, 1)
                dve.tensor_scalar(scale[:, 1, :], scale[:, 0, :], 0.5, None, ALU.mult).then_inc(scaled, 1)
                dve.tensor_scalar(scale[:, 2, :], scale[:, 0, :], -0.5, None, ALU.mult).then_inc(scaled, 1)

            def ternary(w, scale, below, tern, m, scaled, cmp, ready):
                if m == 0:
                    dve.wait_ge(scaled, 3)
                dve.tensor_scalar(below[:, m, :], w[:, m, :], scale[:, 2, m:m + 1], None,
                                  ALU.is_lt).then_inc(cmp, 1)
                dve.wait_ge(cmp, m + 1)
                dve.scalar_tensor_tensor(tern[:, m, :], w[:, m, :], scale[:, 1, m:m + 1], below[:, m, :],
                                         ALU.is_gt, ALU.subtract).then_inc(ready, 1)

            scales(fc_sum, fc_scale, KH, E, fc_summed, fc_scaled)
            for m in range(KH):
                ternary(fc_sb, fc_scale, fc_below, fc_tern, m, fc_scaled, fc_cmp, fc_ternary)

            dve.wait_ge(rows_in, 32)
            dve.wait_ge(small_in, 16 * SMALL_LOADS)
            dve.reciprocal(fc_scale[:, 3, :], fc_scale[:, 0, :]).then_inc(u_step, 1)
            dve.wait_ge(u_step, 1)
            recip = fc_scale[:, 3, :].rearrange("p (m o) -> p m o", o=1).broadcast_to([P, KH, RANK])
            dve.scalar_tensor_tensor(u_scaled[:, :, :], u_sb[:, :, :], rows_sb[:, R_GATE:R_GATE + 1],
                                     recip, ALU.mult, ALU.mult).then_inc(u_step, 1)
            dve.wait_ge(u_step, 2)
            dve.tensor_copy(u_parts[:, :, 0, :], u_scaled[:, :, :]).then_inc(u_step, 1)
            dve.tensor_copy(u_parts[:, :, 2, :], u_scaled[:, :, :]).then_inc(u_step, 1)
            dve.wait_ge(u_step, 4)
            for part in (1, 3):
                dve.tensor_tensor(u_parts[:, :, part, :], u_scaled[:, :, :],
                                  u_parts[:, :, part - 1, :].bitcast(F32), ALU.subtract).then_inc(u_step, 1)
            for g in range(GRP):
                dve.scalar_tensor_tensor(alibi[:, g, :], rel, slope_sb[:, g:g + 1], neg, ALU.mult,
                                         ALU.add).then_inc(alibi_done, 1)

            def norm(f, which, hidden_state, ps, other, src_done, src_count, h_sem, bn_sem, var_sem, std_sem,
                     rstd_sem, z_sem):
                for b in range(f * BH, (f + 1) * BH):
                    dve.wait_ge(src_done, src_count(b))
                    dve.tensor_tensor(hidden_state[:, b, :], ps(b), other(b), ALU.add).then_inc(h_sem, 1)
                    dve.wait_ge(h_sem, b + 1)
                    dve.bn_stats(bn6[:, which, b, :], hidden_state[:, b, :]).then_inc(bn_sem, 1)
                    dve.wait_ge(bn_sem, b + 1)
                    dve.bn_aggr(mv[:, which, b, :], bn6[:, which, b, :]).then_inc(var_sem, 1)
                dve.wait_ge(std_sem, f + 1)
                dve.reciprocal(rstd[:, which, f * BH:(f + 1) * BH],
                               std[:, which, f * BH:(f + 1) * BH]).then_inc(rstd_sem, 1)
                dve.wait_ge(rstd_sem, f + 1)
                for b in range(f * BH, (f + 1) * BH):
                    dve.tensor_scalar(z[:, b, :], hidden_state[:, b, :], mv[:, which, b, 0:1],
                                      rstd[:, which, b:b + 1], ALU.subtract, ALU.mult).then_inc(z_sem, 1)

            def low_part(dst, src, hi, count, hi_ready, signal):
                dve.wait_ge(hi_ready, count)
                dve.tensor_tensor(dst, src, hi.bitcast(F32), ALU.subtract).then_inc(signal, 1)

            def norm1(f):
                norm(f, 0, h1, lambda b: tok_ps[b], lambda b: posb[:, :], tok_done, lambda b: b + 1, h1_ready, bn1, var1,
                     std1, rstd1, z1_ready)

            dve.wait_ge(posb_done, 1)
            norm1(0)
            norm1(1)
            for f in range(HALVES):
                low_part(zt_lo[f][:, :, :], zt_ps[f][:, :].rearrange("p (k t) -> p k t", k=KE),
                         zt_hi[f][:, :, :], f + 1, zt_hi_ready, zt_lo_ready)
            scales(mlp_sum, mlp_scale, KE, HID, mlp_summed, mlp_scaled)
            for o in range(KE):
                ternary(mlp_sb, mlp_scale, mlp_below, mlp_tern, o, mlp_scaled, mlp_cmp, mlp_ternary)

            def spread(f, dst, src, ready, count, signal):
                dve.wait_ge(ready, count)
                for a in range(SPREAD_DVE):
                    last = dve.tensor_scalar(dst[:, f, :, a, :], src, mask[:, a:a + 1], None, ALU.mult)
                last.then_inc(signal, 1)

            def q_strips(f):
                src = q_t[:, f, :, :].rearrange("p g (i s) -> p (g i) s", s=S)
                spread(f, q_spread, src, q_ready, GRP * (f + 1), q_spread_dve)

            def p_strips(f):
                spread(f, p_spread, p_t[:, f, :, :], pt_ready, f + 1, p_spread_dve)

            def values_out(f):
                dve.wait_ge(v_done, f + 1)
                bias = rows_sb[:, R_VB:R_VB + E].rearrange("p (o e) -> p o e", o=1)
                dve.tensor_tensor(v_tok[:, f, :, :], v_ps[f][:, :].rearrange("p (b e) -> p b e", b=BH),
                                  bias.broadcast_to([P, BH, E]), ALU.add).then_inc(v_ready, 1)

            for f in range(HALVES):
                q_strips(f)
                values_out(f)

            def per_key(t, f):
                return t[:, f, :].rearrange("p (n o) -> p n o", o=1).broadcast_to([P, GRP * IPH, S])

            def softmax_shift(f):
                dve.wait_ge(alibi_done, GRP)
                dve.wait_ge(s_done, f + 1)
                for g in range(GRP):
                    ab = alibi[:, g, :].rearrange("p (o s) -> p o s", o=1).broadcast_to([P, IPH, S])
                    src = s_ps[f][:, g * HT:(g + 1) * HT].rearrange("p (i s) -> p i s", s=S)
                    dve.scalar_tensor_tensor(score[:, f, g, :, :], src, float(D) ** -0.5, ab, ALU.mult,
                                             ALU.add).then_inc(score_ready, 1)
                dve.wait_ge(score_ready, GRP * (f + 1))
                rows_ = score[:, f, :, :, :].rearrange("p g i s -> p (g i) s")
                dve.tensor_reduce(smax[:, f, :], rows_, AX.X, ALU.max).then_inc(max_ready, 1)
                dve.wait_ge(max_ready, f + 1)
                dve.tensor_tensor(shifted[:, f, :, :], rows_, per_key(smax, f),
                                  ALU.subtract).then_inc(shift_ready, 1)

            def softmax_norm(f):
                dve.wait_ge(exp_ready, f + 1)
                dve.tensor_reduce(ssum[:, f, :], expd[:, f, :, :], AX.X, ALU.add).then_inc(sum_ready, 1)
                dve.wait_ge(sum_ready, f + 1)
                dve.reciprocal(srec[:, f, :], ssum[:, f, :]).then_inc(rec_ready, 1)
                dve.wait_ge(rec_ready, f + 1)
                dve.tensor_tensor(prob[:, f, :, :].rearrange("p g (i s) -> p (g i) s", s=S),
                                  expd[:, f, :, :], per_key(srec, f), ALU.mult).then_inc(prob_ready, 1)

            softmax_shift(0)
            softmax_norm(0)
            softmax_shift(1)
            p_strips(0)
            softmax_norm(1)
            p_strips(1)
            for f in range(HALVES):
                low_part(yt_lo[f][:, :, :], yt_ps[f][:, :].rearrange("p (g t) -> p g t", g=GRP),
                         yt_hi[f][:, :, :], f + 1, yt_hi_ready, yt_lo_ready)
            dve.wait_ge(h1b_ready, BLOCKS)
            for f in range(HALVES):
                norm(f, 1, h2, lambda b: o_ps[b // BH][:, (b % BH) * E:(b % BH + 1) * E],
                     lambda b: h1b[:, b, :], o_done, lambda b: b // BH + 1, h2_ready, bn2, var2, std2, rstd2, z2_ready)
                low_part(z2t_lo[f][:, :, :], z2t_ps[f][:, :].rearrange("p (k t) -> p k t", k=KE),
                         z2t_hi[f][:, :, :], f + 1, z2t_hi_ready, z2t_lo_ready)
                dve.wait_ge(low_a_done, f + 1)
                dve.tensor_copy(low_a[:, f, :], low_ps[f][0:2 * RANK, 0:HT]).then_inc(low_a_ready, 1)
                dve.wait_ge(low_hi_ready, f + 1)
                dve.tensor_tensor(low_t[2 * RANK:4 * RANK, f, :], low_ps[f][2 * RANK:4 * RANK, HT:2 * HT],
                                  low_t[2 * RANK:4 * RANK, f, :].bitcast(F32),
                                  ALU.subtract).then_inc(low_ready, 1)

            def result(f):
                dve.wait_ge(mlp_step, PAIRS * (f + 1))
                dve.wait_ge(h2t_ready, f + 1)
                for m in range(KE):
                    dve.scalar_tensor_tensor(out_sb[:, f, m, :], mlp_ps[f][:, m * HT:(m + 1) * HT],
                                             mlp_scale[:, 0, m:m + 1], h2_t[:, f, m, :], ALU.mult,
                                             ALU.add).then_inc(out_ready, 1)

            for n in range(HALVES * PAIRS):
                r = n % RING
                dve.wait_ge(relu_ready, 2 * n + 2)
                if n >= RING:
                    dve.wait_ge(mlp_step, n - RING + 1)
                dve.tensor_tensor(sq[:, r, :, :], relu[:, r, :, :], relu[:, r, :, :],
                                  ALU.mult).then_inc(sq_ready, 1)
                dve.wait_ge(sq_ready, n + 1)
                low_part(sq_lo[:, r, :, :], sq[:, r, :, :], sq_hi[:, r, :, :], n + 1, sq_hi_ready,
                         sq_lo_ready)
                if n == PAIRS + 1:
                    result(0)
            result(1)

        @block.gpsimd
        def _(pool):
            def split(w, hi, lo, signal):
                pool.tensor_scalar(hi, w, 1.0, 1.0, ALU.mult, ALU.mult).then_inc(signal, 1)
                pool.wait_ge(signal, 1)
                pool.tensor_tensor(lo, w, hi.bitcast(F32), ALU.subtract).then_inc(signal, 1)

            pool.wait_ge(rows_in, 32)
            pool.tensor_tensor(posb[:, :], pos_sb[:, :], rows_sb[:, R_TOKB:R_TOKB + E],
                               ALU.add).then_inc(posb_done, 1)
            pool.wait_ge(kqv_in, 16)
            split(kqv_sb[:, :, :], kqv_hi[:, :, :], kqv_lo[:, :, :], kqv_split)
            pool.wait_ge(proj_in, 16)
            split(proj_sb[:, :, :], proj_hi[:, :, :], proj_lo[:, :, :], proj_split)
            for b in range(BLOCKS):
                pool.wait_ge(h1_ready, b + 1)
                pool.tensor_tensor(h1b[:, b, :], h1[:, b, :], rows_sb[:, R_PB:R_PB + E],
                                   ALU.add).then_inc(h1b_ready, 1)
            pool.wait_ge(small_in, 16 * SMALL_LOADS)
            split(v_sb[:, :, :], v_parts[:, :, 0, :], v_parts[:, :, 1, :], v_split)


def shape_constants():
    p = np.arange(P)
    key, query = np.arange(S)[None, :], (p % S)[:, None]
    c = np.zeros((P, C_END), np.float32)
    c[:, C_ID:C_ID + P] = np.eye(P)
    c[:, C_MASK:C_MASK + 8] = p[:, None] // 16 == np.arange(8)[None, :]
    c[:, C_REL:C_REL + S] = np.where(key <= query, key - query, 0)
    c[:, C_NEG:C_NEG + S] = np.where(key > query, NEG_INF, 0.0)
    return c


def kernel(x, L0_tok_W, L0_tok_b, L0_tok_pos_emb, L0_attn_W_kqv, L0_attn_b_kqv, L0_attn_W_proj,
           L0_attn_b_proj, L0_attn_slopes, L0_ffn_fast_b, L0_ffn_w_fc, L0_ffn_w_proj, L0_ffn_u,
           L0_ffn_v, L0_ffn_gate):
    import concourse.bacc as bacc
    from concourse.bass_utils import run_bass_kernel_spmd

    a = np.asarray
    patches = a(x).reshape(IMAGES, CH, SIDE, PATCH, SIDE, PATCH).transpose(1, 3, 5, 0, 2, 4)
    b_kqv = a(L0_attn_b_kqv)
    arrays = {
        "x_t": patches.reshape(FEAT, TOK),
        "wtok_t": a(L0_tok_W).T,
        "consts": shape_constants(),
        "rows": np.concatenate([a(L0_tok_b), b_kqv[2 * E:], a(L0_attn_b_proj),
                                a(L0_ffn_gate).reshape(1)]).reshape(1, R_END),
        "pos": np.tile(a(L0_tok_pos_emb), (IPB, 1)),
        "w_kqv": a(L0_attn_W_kqv),
        "qk_bias": b_kqv[:2 * E].reshape(2 * GRP, P).T,
        "slopes": np.repeat(a(L0_attn_slopes).reshape(GRP, HPG), S, axis=1).T,
        "w_proj": a(L0_attn_W_proj),
        "w_fc": a(L0_ffn_w_fc),
        "w_mlp": a(L0_ffn_w_proj),
        "u_nat": a(L0_ffn_u),
        "v_t": a(L0_ffn_v).T,
        "fb_t": a(L0_ffn_fast_b).T,
    }
    arrays = {n: np.ascontiguousarray(t) for n, t in arrays.items()}
    nc = bacc.Bacc("TRN2", target_bir_lowering=False, num_devices=1)
    args = {n: nc.dram_tensor(n, t.shape, mybir.dt.from_np(t.dtype), kind="ExternalInput").ap()
            for n, t in arrays.items()}
    out_t = nc.dram_tensor("out_t", (E, TOK), F32, kind="ExternalOutput").ap()
    build_program(nc, out_t=out_t, **args)
    got = run_bass_kernel_spmd(nc, [arrays], core_ids=[0])
    return a(got.results[0]["out_t"]).T.reshape(IMAGES, S, E)
```

```python
from contextlib import ExitStack

import numpy as np

import concourse.bass as bass
from concourse import mybir

F32 = mybir.dt.float32
F32R = mybir.dt.float32r
BF16 = mybir.dt.bfloat16
ALU = mybir.AluOpType
ACT = mybir.ActivationFunctionType
AX = mybir.AxisListType

P = 128
IMAGES, CH, IMG, PATCH = 32, 3, 64, 16
SIDE = IMG // PATCH
S = SIDE * SIDE
TOK = IMAGES * S
FEAT = CH * PATCH * PATCH
E = 256
H, D = 16, 16
HID, RANK = 1024, 16
KF, KE, KH = FEAT // P, E // P, HID // P
HALVES = 2
HT = TOK // HALVES
BH = HT // P
BLOCKS = TOK // P
IPB = P // S
HPG = P // D
GRP = H // HPG
IPH = IMAGES // HALVES
NEG_INF = -1e30
EPS = 1e-5
SPREAD_DVE = 6

C_ID, C_MASK, C_REL, C_NEG = 0, P, P + 8, P + 8 + S
C_END = C_NEG + S
R_TOKB, R_GATE = 0, E
R_END = E + 1
PARTS = 3


def build_program(nc, x_t, wtok_t, consts, rows, pos, w_kqv, bias_row, slopes, w_proj, w_fc, w_mlp,
                  u_nat, v_t, fb_t, out_t):
    with ExitStack() as ctx:
        def sb(name, shape, dt=F32):
            return ctx.enter_context(nc.sbuf_tensor(name, shape, dt))

        def sem(name):
            return ctx.enter_context(nc.semaphore(name))

        bank = [ctx.enter_context(nc.psum_tensor(f"bank{i}", [P, 512], F32)) for i in range(8)]

        x_sb = sb("x_sb", [P, KF, TOK])
        wtok_sb = sb("wtok_sb", [P, KF, E])
        const_sb = sb("const_sb", [P, C_END])
        rows_sb = sb("rows_sb", [P, R_END])
        pos_sb = sb("pos_sb", [P, E])
        kqv_sb = sb("kqv_sb", [P, KE, 3 * E])
        bias_sb = sb("bias_sb", [64, 4 * E])
        slope_sb = sb("slope_sb", [P, GRP])
        proj_sb = sb("proj_sb", [P, KE, E])
        fc_sb = sb("fc_sb", [P, KH, E])
        mlp_sb = sb("mlp_sb", [P, KE, HID])
        u_sb = sb("u_sb", [P, KH, RANK])
        v_sb = sb("v_sb", [P, KE, RANK])
        fb_sb = sb("fb_sb", [2 * RANK, 4 * RANK])

        ident = const_sb[:, C_ID:C_ID + P]
        mask = const_sb[:, C_MASK:C_MASK + 8]
        rel = const_sb[:, C_REL:C_REL + S]
        neg = const_sb[:, C_NEG:C_NEG + S]

        ident_bf = sb("ident_bf", [P, P], BF16)
        posb = pos_sb
        alibi = sb("alibi", [P, GRP, S])
        bias_parts = sb("bias_parts", [64, 4 * E], F32R)
        ones_f = sb("ones_f", [64, HT])
        ones = sb("ones", [64, HT], F32R)
        kqv_hi = sb("kqv_hi", [P, KE, 3 * E], F32R)
        kqv_lo = sb("kqv_lo", [P, KE, 3 * E], F32R)
        proj_hi = sb("proj_hi", [P, KE, E], F32R)
        proj_lo = sb("proj_lo", [P, KE, E], F32R)
        v_parts = sb("v_parts", [P, KE, 2, RANK], F32R)
        fc_sum = sb("fc_sum", [P, KH])
        mlp_sum = sb("mlp_sum", [P, KE])
        fc_scale = sb("fc_scale", [P, 4, KH])
        mlp_scale = sb("mlp_scale", [P, 3, KE])
        fc_tern = sb("fc_tern", [P, KH, E], BF16)
        mlp_tern = sb("mlp_tern", [P, KE, HID], BF16)
        fc_t = sb("fc_t", [P, KE, HID], F32R)
        mlp_t = sb("mlp_t", [P, KH, E], F32R)
        u_scaled = sb("u_scaled", [P, KH, RANK])
        u_parts = sb("u_parts", [P, KH, 4, RANK], F32R)
        u_t = sb("u_t", [4 * RANK, HID], F32R)
        eps_sb = sb("eps_sb", [P, 1])
        table_junk = sb("table_junk", [P, 1])

        h1 = sb("h1", [P, BLOCKS, E])
        h2 = h1
        bn6 = sb("bn6", [P, 2, BLOCKS, 6])
        mv = sb("mv", [P, 2, BLOCKS, 2])
        std = sb("std", [P, 2, BLOCKS])
        rstd = sb("rstd", [P, 2, BLOCKS])
        z = sb("z", [P, BLOCKS, E])
        zt_hi = [sb(f"zt_hi{f}", [P, KE, HT], F32R) for f in range(HALVES)]
        zt_lo = [sb(f"zt_lo{f}", [P, KE, HT], F32R) for f in range(HALVES)]
        q_part = sb("q_part", [P, HALVES, PARTS, GRP * IPH, S], BF16)
        k_part = sb("k_part", [P, HALVES, PARTS, GRP * IPH, S], BF16)
        v_part = sb("v_part", [P, HALVES, PARTS, BH * H, D], BF16)
        p_part = sb("p_part", [P, HALVES, PARTS, BH * H, S], BF16)
        q_spread = sb("q_spread", [P, HALVES, PARTS, GRP * IPH, HPG, S], BF16)
        p_spread = q_spread
        abs_junk = p_part[:, 0, 0, 0:E // S, :].rearrange("p n s -> p (n s)")
        mlp_junk = mlp_tern[:, 0, :]
        smax = sb("smax", [P, HALVES, GRP * IPH])
        ssum = sb("ssum", [P, HALVES, GRP * IPH])
        srec = sb("srec", [P, HALVES, GRP * IPH])

        def reuse(base, lot):
            flat = base[:, :, :].rearrange("p k n -> p (k n)")
            return flat[:, lot * HALVES * 2 * HT:(lot + 1) * HALVES * 2 * HT]

        score = reuse(x_sb, 0).rearrange("p (f g i s) -> p f g i s", f=HALVES, g=GRP, s=S)
        prob = reuse(x_sb, 0).rearrange("p (f g n) -> p f g n", f=HALVES, g=GRP)
        y_tok = reuse(x_sb, 0).rearrange("p (f b e) -> p f b e", f=HALVES, b=BH)
        shifted = reuse(x_sb, 1).rearrange("p (f n s) -> p f n s", f=HALVES, s=S)
        expd = reuse(x_sb, 2).rearrange("p (f n s) -> p f n s", f=HALVES, s=S)
        rest = reuse(wtok_sb, 0).rearrange("p (f n s) -> p f n s", f=HALVES, s=S)
        h2_t = reuse(mlp_sb, 1).rearrange("p (f k t) -> p f k t", f=HALVES, k=KE)
        yt_hi, yt_lo, z2t_hi, z2t_lo = zt_hi, zt_lo, zt_hi, zt_lo
        low_a = y_tok[0:2 * RANK, :, 0, :]
        low_t = sb("low_t", [4 * RANK, HALVES, HT], F32R)
        RING = 3
        relu = wtok_sb[:, :, :].rearrange("p (r a) t -> p r a t", a=2)
        sq = kqv_sb[:, :, :].rearrange("p k n -> p (k n)").rearrange("p (r a t) -> p r a t", r=RING, a=2)
        sq_hi = sb("sq_hi", [P, RING, 2, HT], F32R)
        sq_lo = sb("sq_lo", [P, RING, 2, HT], F32R)
        out_sb = reuse(x_sb, 0).rearrange("p (f k t) -> p f k t", f=HALVES, k=KE)
        rest_k = expd
        rest_v = reuse(kqv_sb, 0).rearrange("p (f n s) -> p f n s", f=HALVES, s=S)

        tok_ps = [bank[b][:, 0:E] for b in range(BLOCKS)]
        zt_ps = [bank[4], bank[5]]
        q_ps = [bank[6], bank[1]]
        k_ps = [bank[7], bank[2]]
        v_ps = [bank[0], bank[3]]
        s_ps = [bank[4], bank[5]]
        pt_ps = [bank[6], bank[7]]
        y_ps = [bank[0], bank[1]]
        fct_ps = [bank[2 + k][:, :].bitcast(BF16) for k in range(KE)]
        mlpt_ps = [bank[2 + i][:, :].bitcast(BF16) for i in range(2)]
        ut_ps = [bank[2 + i][0:4 * RANK, :] for i in range(2)]
        yt_ps = [bank[4], bank[5]]
        o_ps = [bank[6], bank[7]]
        z2t_ps = [bank[0], bank[1]]
        h2t_ps = [bank[4], bank[5]]
        low_ps = [bank[6], bank[7]]
        FCB = [bank[2], bank[3], bank[0], bank[6]]
        mlp_ps = [bank[4], bank[5]]

        tok_in = [sem(f"tok_in{k}") for k in range(KF)]
        x2_in = [sem(f"x2_in{i}") for i in range(2)]
        const_in = sem("const_in")
        rows_in = sem("rows_in")
        q_in, k_in, v_in = sem("q_in"), sem("k_in"), sem("v_in")
        slope_in = sem("slope_in")
        bias_in = sem("bias_in")
        small_in = sem("small_in")
        proj_in = sem("proj_in")
        fc_in = sem("fc_in")
        mlp_in = sem("mlp_in")
        out_done = sem("out_done")
        eps_set = sem("eps_set")
        identbf_done = sem("identbf_done")
        posb_done = sem("posb_done")
        alibi_done = sem("alibi_done")
        q_w_hi, k_w_hi, v_w_hi = sem("q_w_hi"), sem("k_w_hi"), sem("v_w_hi")
        q_split, k_split, v_w_split = sem("q_split"), sem("k_split"), sem("v_w_split")
        proj_split = sem("proj_split")
        v_split = sem("v_split")
        fc_summed = sem("fc_summed")
        mlp_summed = sem("mlp_summed")
        fc_scaled = sem("fc_scaled")
        mlp_scaled = sem("mlp_scaled")
        fc_cmp = sem("fc_cmp")
        fc_ternary = sem("fc_ternary")
        mlp_cmp = sem("mlp_cmp")
        mlp_ternary = sem("mlp_ternary")
        fct_turned = sem("fct_turned")
        fct_ready = sem("fct_ready")
        mlpt_turned = sem("mlpt_turned")
        mlpt_ready = sem("mlpt_ready")
        u_step = sem("u_step")
        ut_turned = sem("ut_turned")
        ut_ready = sem("ut_ready")
        tok_done = sem("tok_done")
        h1_ready = sem("h1_ready")
        bias_set = sem("bias_set")
        ones_set = sem("ones_set")
        bn1 = sem("bn1")
        var1 = sem("var1")
        std1 = sem("std1")
        rstd1 = sem("rstd1")
        z1_ready = sem("z1_ready")
        zt_turned = sem("zt_turned")
        zt_hi_ready = sem("zt_hi_ready")
        zt_lo_ready = sem("zt_lo_ready")
        q_done = sem("q_done")
        k_done = sem("k_done")
        v_done = sem("v_done")
        q_first, q_rest, q_second, q_ready = (sem(f"q_{n}") for n in ("first", "rest", "second", "ready"))
        k_first, k_rest, k_second, k_ready = (sem(f"k_{n}") for n in ("first", "rest", "second", "ready"))
        v_first, v_rest, v_second, v_ready = (sem(f"v_{n}") for n in ("first", "rest", "second", "ready"))
        p_first, p_rest, p_second, p_ready = (sem(f"p_{n}") for n in ("first", "rest", "second", "ready"))
        q_spread_dve = sem("q_spread_dve")
        q_spread_act = sem("q_spread_act")
        s_done = sem("s_done")
        score_ready = sem("score_ready")
        max_ready = sem("max_ready")
        shift_ready = sem("shift_ready")
        exp_ready = sem("exp_ready")
        sum_ready = sem("sum_ready")
        rec_ready = sem("rec_ready")
        prob_ready = sem("prob_ready")
        pt_turned = sem("pt_turned")
        p_spread_dve = sem("p_spread_dve")
        p_spread_act = sem("p_spread_act")
        y_done = sem("y_done")
        y_ready = sem("y_ready")
        yt_turned = sem("yt_turned")
        yt_hi_ready = sem("yt_hi_ready")
        yt_lo_ready = sem("yt_lo_ready")
        o_done = sem("o_done")
        h2_ready = sem("h2_ready")
        bn2 = sem("bn2")
        var2 = sem("var2")
        std2 = sem("std2")
        rstd2 = sem("rstd2")
        z2_ready = sem("z2_ready")
        z2t_turned = sem("z2t_turned")
        h2t_turned = sem("h2t_turned")
        h2t_ready = sem("h2t_ready")
        z2t_hi_ready = sem("z2t_hi_ready")
        z2t_lo_ready = sem("z2t_lo_ready")
        low_a_done = sem("low_a_done")
        low_a_ready = sem("low_a_ready")
        low_c_done = sem("low_c_done")
        low_hi_ready = sem("low_hi_ready")
        low_ready = sem("low_ready")
        fc_done = sem("fc_done")
        relu_ready = sem("relu_ready")
        sq_ready = sem("sq_ready")
        sq_hi_ready = sem("sq_hi_ready")
        sq_lo_ready = sem("sq_lo_ready")
        mlp_step = sem("mlp_step")
        mlp_done = sem("mlp_done")
        out_ready = sem("out_ready")

        block = ctx.enter_context(nc.Block())
        SMALL_LOADS = 4
        PAIRS = KH // 2

        @block.sync
        def _(sp):
            for k in range(KF):
                sp.dma_start(x_sb[:, k, 0:HT], x_t[k * P:(k + 1) * P, 0:HT]).then_inc(tok_in[k], 16)
                sp.dma_start(wtok_sb[:, k, :], wtok_t[k * P:(k + 1) * P, :]).then_inc(tok_in[k], 16)
            half = KF // 2
            for i in range(2):
                sp.dma_start(x_sb[:, i * half:(i + 1) * half, HT:TOK],
                             x_t[i * half * P:(i + 1) * half * P, HT:TOK].rearrange("(k p) t -> p k t", p=P)
                             ).then_inc(x2_in[i], 16)
            for which, signal in ((1, q_in), (0, k_in), (2, v_in)):
                c = which * E
                sp.dma_start(kqv_sb[:, :, c:c + E], w_kqv[:, c:c + E].rearrange("(k p) n -> p k n", p=P)
                             ).then_inc(signal, 16)
            sp.dma_start(proj_sb[:, :, :], w_proj.rearrange("(k p) n -> p k n", p=P)).then_inc(proj_in, 16)
            sp.dma_start(fc_sb[:, :, :], w_fc.rearrange("(m p) e -> p m e", p=P)).then_inc(fc_in, 16)
            sp.dma_start(mlp_sb[:, :, :], w_mlp.rearrange("(k p) n -> p k n", p=P)).then_inc(mlp_in, 16)
            for f in range(HALVES):
                for m in range(KE):
                    sp.wait_ge(out_ready, f * KE + m + 1)
                    sp.dma_start(out_t[m * P:(m + 1) * P, f * HT:(f + 1) * HT],
                                 out_sb[:, f, m, :]).then_inc(out_done, 16)
            sp.wait_ge(out_done, 16 * HALVES * KE)

        @block.tensor
        def _(pe):
            def split_product(out, pairs, start=True):
                for i, (lhs, rhs) in enumerate(pairs):
                    mm = pe.matmul(out, lhs, rhs, start=start and i == 0, stop=i == len(pairs) - 1)
                return mm

            def embed(k, b):
                return pe.matmul(tok_ps[b], x_sb[:, k, b * P:(b + 1) * P], wtok_sb[:, k, :],
                                 start=k == 0, stop=k == KF - 1)

            def turn_z(f, src, dst, ready, signal):
                for b in range(BH):
                    pe.wait_ge(ready, f * BH + b + 1)
                    for k in range(KE):
                        mm = pe.transpose(dst[:, k * HT + b * P:k * HT + (b + 1) * P],
                                          src(f * BH + b)[:, k * P:(k + 1) * P], ident)
                mm.then_inc(signal, 1)

            def query_key(f, which, ps, weights, signal):
                pe.wait_ge(weights, 1)
                pe.wait_ge(bias_set, 4)
                pe.wait_ge(ones_set, 2)
                pe.wait_ge(zt_hi_ready, f + 1)
                pe.wait_ge(zt_lo_ready, f + 1)
                for g in range(GRP):
                    c = which * E + g * P
                    pairs = [(bias_parts[:, c:c + P], ones[:, :])]
                    for k in range(KE):
                        hi, lo = kqv_hi[:, k, c:c + P], kqv_lo[:, k, c:c + P]
                        pairs += [(hi, zt_hi[f][:, k, :]), (hi, zt_lo[f][:, k, :]),
                                  (lo, zt_hi[f][:, k, :])]
                    mm = split_product(ps[f][:, g * HT:(g + 1) * HT], pairs)
                mm.then_inc(signal, 1)

            def value_product(f):
                pe.wait_ge(v_w_split, 1)
                for b in range(BH):
                    pairs = [(ones[:, 0:P], bias_parts[:, 2 * E:3 * E])]
                    for k in range(KE):
                        zh, zl = (t[f][:, k, b * P:(b + 1) * P] for t in (zt_hi, zt_lo))
                        wh, wl = (t[:, k, 2 * E:3 * E] for t in (kqv_hi, kqv_lo))
                        pairs += [(zh, wh), (zh, wl), (zl, wh)]
                    mm = split_product(v_ps[f][:, b * E:(b + 1) * E], pairs)
                mm.then_inc(v_done, 1)

            def bf16_product(out, lhs, rhs):
                order = [(i, n - i) for n in range(PARTS - 1, -1, -1) for i in range(n + 1)]
                return split_product(out, [(lhs(i), rhs(j)) for i, j in order])

            def scores(f, g):
                pe.wait_ge(k_ready, f + 1)
                pe.wait_ge(q_spread_dve, GRP * f + g + 1)
                pe.wait_ge(q_spread_act, GRP * f + g + 1)
                for gi in range(g * IPH, (g + 1) * IPH):
                    mm = bf16_product(s_ps[f][:, gi * S:(gi + 1) * S],
                                      lambda i: q_spread[:, f, i, gi, :, :],
                                      lambda j: k_part[:, f, j, gi, :])
                mm.then_inc(s_done, 1)

            def turn_probs(f):
                pe.wait_ge(prob_ready, f + 1)
                for b in range(BH):
                    for g in range(GRP):
                        c = (b * GRP + g) * P
                        mm = pe.transpose(pt_ps[f][:, c:c + P], prob[:, f, g, b * P:(b + 1) * P], ident)
                mm.then_inc(pt_turned, 1)

            def values(f, b):
                pe.wait_ge(v_ready, f + 1)
                pe.wait_ge(p_spread_dve, BH * f + b + 1)
                pe.wait_ge(p_spread_act, BH * f + b + 1)
                for bh in range(b * H, (b + 1) * H):
                    mm = bf16_product(y_ps[f][:, bh * D:(bh + 1) * D],
                                      lambda i: p_spread[:, f, i, bh, :, :],
                                      lambda j: v_part[:, f, j, bh, :])
                mm.then_inc(y_done, 1)

            def turn_y(f):
                pe.wait_ge(y_ready, f + 1)
                for b in range(BH):
                    for g in range(GRP):
                        c = g * HT + b * P
                        mm = pe.transpose(yt_ps[f][:, c:c + P], y_tok[:, f, b, g * P:(g + 1) * P], ident)
                mm.then_inc(yt_turned, 1)

            def project(f):
                pe.wait_ge(proj_split, 2)
                pe.wait_ge(yt_hi_ready, f + 1)
                pe.wait_ge(yt_lo_ready, f + 1)
                for b in range(BH):
                    pairs = [(ones[:, 0:P], bias_parts[:, 3 * E:4 * E])]
                    for g in range(GRP):
                        yh, yl = (t[f][:, g, b * P:(b + 1) * P] for t in (yt_hi, yt_lo))
                        pairs += [(yh, proj_hi[:, g, :]), (yh, proj_lo[:, g, :]), (yl, proj_hi[:, g, :])]
                    mm = split_product(o_ps[f][:, b * E:(b + 1) * E], pairs)
                mm.then_inc(o_done, 1)

            def low_rank_a(f):
                pe.wait_ge(v_split, 2)
                pe.wait_ge(z2t_hi_ready, f + 1)
                pe.wait_ge(z2t_lo_ready, f + 1)
                pairs = []
                for k in range(KE):
                    vp = v_parts[:, k, :, :]
                    pairs += [(vp, z2t_hi[f][:, k, :]), (vp, z2t_lo[f][:, k, :])]
                split_product(low_ps[f][0:2 * RANK, 0:HT], pairs).then_inc(low_a_done, 1)

            def low_rank_c(f):
                pe.wait_ge(low_a_ready, f + 1)
                pe.wait_ge(small_in, 16 * SMALL_LOADS)
                pe.matmul(low_ps[f][0:4 * RANK, HT:2 * HT], fb_sb[:, :], low_a[:, f, :],
                          start=True, stop=True).then_inc(low_c_done, 1)

            def hidden(f, j):
                n = f * PAIRS + j
                if n >= len(FCB):
                    pe.wait_ge(relu_ready, 2 * (n - len(FCB) + 1))
                ps = FCB[n % len(FCB)]
                for a in range(2):
                    m = 2 * j + a
                    out = ps[:, a * HT:(a + 1) * HT]
                    pairs = []
                    for k in range(KE):
                        w = fc_t[:, k, m * P:(m + 1) * P]
                        pairs += [(w, z2t_hi[f][:, k, :]), (w, z2t_lo[f][:, k, :])]
                    for i, (lhs, rhs) in enumerate(pairs):
                        pe.matmul(out, lhs, rhs, start=i == 0, stop=False)
                    if j == 0 and a == 0:
                        pe.wait_ge(low_ready, f + 1)
                    mm = pe.matmul(out, u_t[:, m * P:(m + 1) * P], low_t[:, f, :], start=False, stop=True)
                mm.then_inc(fc_done, 1)

            def mlp_out(f, j):
                n = f * PAIRS + j
                pe.wait_ge(sq_hi_ready, n + 1)
                pe.wait_ge(sq_lo_ready, n + 1)
                for a in range(2):
                    for m in range(KE):
                        w = mlp_t[:, 2 * j + a, m * P:(m + 1) * P]
                        for i, part in enumerate((sq_hi, sq_lo)):
                            first = j == 0 and a == 0 and i == 0
                            mm = pe.matmul(mlp_ps[f][:, m * HT:(m + 1) * HT], w,
                                           part[:, n % RING, a, :], start=first and m == 0,
                                           stop=j == PAIRS - 1 and a == 1 and i == 1,
                                           skip_group_check=True)
                mm.then_inc(mlp_step, 1)

            def turn_fc():
                pe.wait_ge(identbf_done, 1)
                pe.wait_ge(fc_ternary, KH)
                for k in range(KE):
                    for m in range(KH):
                        mm = pe.transpose(fct_ps[k][:, m * P:(m + 1) * P],
                                          fc_tern[:, m, k * P:(k + 1) * P], ident_bf[:, :])
                    mm.then_inc(fct_turned, 1)

            def turn_mlp():
                pe.wait_ge(mlp_ternary, KE)
                for i in range(2):
                    pe.wait_ge(fct_ready, i + 1)
                    for m in range(4):
                        for o in range(KE):
                            c = (m * KE + o) * P
                            mm = pe.transpose(mlpt_ps[i][:, c:c + P],
                                              mlp_tern[:, o, (4 * i + m) * P:(4 * i + m + 1) * P],
                                              ident_bf[:, :])
                    mm.then_inc(mlpt_turned, 1)

            def turn_u():
                pe.wait_ge(u_step, 6)
                for i in range(2):
                    pe.wait_ge(mlpt_ready, i + 1)
                    for m in range(4):
                        mm = pe.transpose(ut_ps[i][:, m * P:(m + 1) * P],
                                          u_parts[:, 4 * i + m, :, :].bitcast(F32), ident)
                    mm.then_inc(ut_turned, 1)

            for k in range(KF):
                pe.wait_ge(tok_in[k], 32)
                for b in range(BH):
                    mm = embed(k, b)
                    if k == KF - 1:
                        mm.then_inc(tok_done, 1)
            for k in range(KF):
                if k % (KF // 2) == 0:
                    pe.wait_ge(x2_in[k // (KF // 2)], 16)
                mm = embed(k, 2)
            mm.then_inc(tok_done, 1)
            for k in range(KF // 2):
                embed(k, 3)
            pe.wait_ge(const_in, 16)
            turn_z(0, lambda b: z[:, b, :], zt_ps[0], z1_ready, zt_turned)
            for k in range(KF // 2, KF):
                mm = embed(k, 3)
            mm.then_inc(tok_done, 1)

            query_key(0, 1, q_ps, q_split, q_done)
            query_key(0, 0, k_ps, k_split, k_done)
            turn_z(1, lambda b: z[:, b, :], zt_ps[1], z1_ready, zt_turned)
            pe.wait_ge(h1_ready, BLOCKS)
            value_product(0)
            query_key(1, 1, q_ps, q_split, q_done)
            query_key(1, 0, k_ps, k_split, k_done)
            for g in range(GRP):
                scores(0, g)
            value_product(1)
            scores(1, 0)
            turn_probs(0)
            scores(1, 1)
            pe.wait_ge(v_first, 2)
            pe.wait_ge(v_rest, 2)
            turn_fc()
            values(0, 0)
            turn_probs(1)
            values(0, 1)
            turn_y(0)
            turn_mlp()
            project(0)
            values(1, 0)
            values(1, 1)
            turn_u()

            def turn_z2(f):
                turn_z(f, lambda b: z[:, b, :], z2t_ps[f], z2_ready, z2t_turned)

            def turn_h2(f):
                turn_z(f, lambda b: h2[:, b, :], h2t_ps[f], h2_ready, h2t_turned)

            turn_z2(0)
            turn_y(1)
            low_rank_a(0)
            project(1)
            low_rank_c(0)
            turn_h2(0)
            pe.wait_ge(fct_ready, KE)
            pe.wait_ge(mlpt_ready, 2)
            pe.wait_ge(ut_ready, 2)
            hidden(0, 0)
            hidden(0, 1)
            turn_z2(1)
            hidden(0, 2)
            pe.wait_ge(h2t_ready, 1)
            mlp_out(0, 0)
            low_rank_a(1)
            turn_h2(1)
            mlp_out(0, 1)
            low_rank_c(1)
            hidden(0, 3)
            mlp_out(0, 2)
            hidden(1, 0)
            mlp_out(0, 3)
            hidden(1, 1)
            pe.wait_ge(h2t_ready, 2)
            mlp_out(1, 0)
            hidden(1, 2)
            mlp_out(1, 1)
            hidden(1, 3)
            mlp_out(1, 2)
            mlp_out(1, 3)

        @block.scalar
        def _(act):
            act.dma_start(const_sb[:, :], consts).then_inc(const_in, 16)
            for r in (0, 32):
                act.dma_start(bias_sb[r:r + 1, :], bias_row).then_inc(bias_in, 16)
            act.wait_ge(eps_set, 1)
            nc.scalar.activation(table_junk[:, :], eps_sb[:, :], ACT.Sqrt)
            act.dma_start(rows_sb[:, :], rows.broadcast_to([P, R_END])).then_inc(rows_in, 16)
            act.dma_start(pos_sb[:, :], pos).then_inc(rows_in, 16)
            act.dma_start(slope_sb[:, :], slopes).then_inc(slope_in, 16)
            act.wait_ge(tok_in[3], 32)
            act.dma_start(u_sb[:, :, :], u_nat.rearrange("(m p) r -> p m r", p=P)).then_inc(small_in, 16)
            act.dma_start(v_sb[:, :, :], v_t.rearrange("(k p) r -> p k r", p=P)).then_inc(small_in, 16)
            for i in range(2):
                act.dma_start(fb_sb[i * RANK:(i + 1) * RANK, :].rearrange("p (a r) -> p a r", a=4),
                              fb_t.rearrange("p (o r) -> p o r", o=1).broadcast_to([RANK, 4, RANK])
                              ).then_inc(small_in, 16)
            act.wait_ge(bias_in, 32)
            act.wait_ge(bias_set, 1)
            for r in (0, 32):
                nc.scalar.activation(bias_parts[r:r + 1, :], bias_sb[r:r + 1, :],
                                     ACT.Copy).then_inc(bias_set, 1)

            def weight_high(which, arrived, ready):
                act.wait_ge(arrived, 16)
                c = which * E
                nc.scalar.activation(kqv_hi[:, :, c:c + E], kqv_sb[:, :, c:c + E],
                                     ACT.Copy).then_inc(ready, 1)

            def fc_sums(tiles):
                act.wait_ge(fc_in, 16)
                for m in tiles:
                    nc.scalar.activation(abs_junk, fc_sb[:, m, :], ACT.Abs,
                                         accum_out=fc_sum[:, m:m + 1]).then_inc(fc_summed, 1)
                    act.wait_ge(fc_summed, m + 1)

            def norm_std(which, var_ready, std_ready, f):
                act.wait_ge(var_ready, BH * (f + 1))
                nc.scalar.activation(std[:, which, f * BH:(f + 1) * BH],
                                     mv[:, which, f * BH:(f + 1) * BH, 1], ACT.Sqrt,
                                     bias=eps_sb[:, 0:1]).then_inc(std_ready, 1)

            def copy_out(dst, src, turned, count, ready):
                act.wait_ge(turned, count)
                nc.scalar.activation(dst, src, ACT.Copy).then_inc(ready, 1)

            weight_high(1, q_in, q_w_hi)
            norm_std(0, var1, std1, 0)
            weight_high(0, k_in, k_w_hi)
            weight_high(2, v_in, v_w_hi)
            copy_out(zt_hi[0][:, :, :], zt_ps[0][:, :], zt_turned, 1, zt_hi_ready)
            norm_std(0, var1, std1, 1)
            act.wait_ge(std1, 2)
            nc.scalar.activation(table_junk[:, :], eps_sb[:, :], ACT.Exp)

            def first_part(dst, f, ps, done, ready):
                act.wait_ge(done, f + 1)
                nc.scalar.activation(dst[:, f, 0, :, :], ps[f][:, :], ACT.Copy).then_inc(ready, 1)

            def spread(f, half, dst, src, ready, signal):
                act.wait_ge(ready, f + 1)
                n = slice(half * IPH, (half + 1) * IPH)
                for a in range(SPREAD_DVE, 8):
                    last = nc.scalar.activation(dst[:, f, :, n, a, :], src[:, f, :, n, :], ACT.Copy,
                                                scale=mask[:, a:a + 1])
                last.then_inc(signal, 1)

            def exponentials(f):
                act.wait_ge(shift_ready, f + 1)
                nc.scalar.activation(expd[:, f, :, :], shifted[:, f, :, :], ACT.Exp).then_inc(exp_ready, 1)

            first_part(q_part, 0, q_ps, q_done, q_first)
            first_part(k_part, 0, k_ps, k_done, k_first)
            copy_out(zt_hi[1][:, :, :], zt_ps[1][:, :], zt_turned, 2, zt_hi_ready)
            for half in range(2):
                fc_sums(range(4 * half, 4 * half + 4))
                spread(0, half, q_spread, q_part, q_ready, q_spread_act)
            first_part(v_part, 0, v_ps, v_done, v_first)
            first_part(q_part, 1, q_ps, q_done, q_first)
            first_part(k_part, 1, k_ps, k_done, k_first)
            for half in range(2):
                spread(1, half, q_spread, q_part, q_ready, q_spread_act)
            act.wait_ge(mlp_in, 16)
            for o in range(KE):
                nc.scalar.activation(mlp_junk, mlp_sb[:, o, :], ACT.Abs,
                                     accum_out=mlp_sum[:, o:o + 1]).then_inc(mlp_summed, 1)
                act.wait_ge(mlp_summed, o + 1)
            first_part(v_part, 1, v_ps, v_done, v_first)
            exponentials(0)
            first_part(p_part, 0, pt_ps, pt_turned, p_first)
            exponentials(1)
            act.wait_ge(exp_ready, 2)
            nc.scalar.activation(table_junk[:, :], eps_sb[:, :], ACT.Sqrt)
            for half in range(2):
                spread(0, half, p_spread, p_part, p_ready, p_spread_act)
            for k in range(KE):
                copy_out(fc_t[:, k, :], fct_ps[k], fct_turned, k + 1, fct_ready)
            first_part(p_part, 1, pt_ps, pt_turned, p_first)
            spread(1, 0, p_spread, p_part, p_ready, p_spread_act)
            copy_out(y_tok[:, 0, :, :], y_ps[0][:, :], y_done, BH, y_ready)
            spread(1, 1, p_spread, p_part, p_ready, p_spread_act)
            copy_out(yt_hi[0][:, :, :], yt_ps[0][:, :], yt_turned, 1, yt_hi_ready)
            for i in range(2):
                copy_out(mlp_t[:, 4 * i:4 * i + 4, :], mlpt_ps[i], mlpt_turned, i + 1, mlpt_ready)
            norm_std(1, var2, std2, 0)
            copy_out(y_tok[:, 1, :, :], y_ps[1][:, :], y_done, 2 * BH, y_ready)
            copy_out(z2t_hi[0][:, :, :], z2t_ps[0][:, :], z2t_turned, 1, z2t_hi_ready)
            copy_out(yt_hi[1][:, :, :], yt_ps[1][:, :], yt_turned, 2, yt_hi_ready)
            for i in range(2):
                copy_out(u_t[:, i * HT * 2:(i + 1) * HT * 2], ut_ps[i], ut_turned, i + 1, ut_ready)

            def low_high(f):
                act.wait_ge(low_c_done, f + 1)
                nc.scalar.activation(low_t[:, f, :], low_ps[f][0:4 * RANK, HT:2 * HT],
                                     ACT.Copy).then_inc(low_hi_ready, 1)

            low_high(0)
            copy_out(h2_t[:, 0, :, :], h2t_ps[0][:, :], h2t_turned, 1, h2t_ready)

            def squares(n):
                f, j = divmod(n, PAIRS)
                if n >= RING:
                    act.wait_ge(sq_ready, n - RING + 1)
                act.wait_ge(fc_done, n + 1)
                for a in range(2):
                    m = 2 * j + a
                    nc.scalar.activation(relu[:, n % RING, a, :], FCB[n % len(FCB)][:, a * HT:(a + 1) * HT],
                                         ACT.Relu, scale=fc_scale[:, 0, m:m + 1]).then_inc(relu_ready, 1)
                if n >= RING:
                    act.wait_ge(mlp_step, n - RING + 1)
                act.wait_ge(relu_ready, 2 * n + 2)
                nc.scalar.activation(sq_hi[:, n % RING, :, :], relu[:, n % RING, :, :],
                                     ACT.Square).then_inc(sq_hi_ready, 1)

            norm_std(1, var2, std2, 1)
            squares(0)
            squares(1)
            copy_out(z2t_hi[1][:, :, :], z2t_ps[1][:, :], z2t_turned, 2, z2t_hi_ready)
            squares(2)
            copy_out(h2_t[:, 1, :, :], h2t_ps[1][:, :], h2t_turned, 2, h2t_ready)
            low_high(1)
            for n in range(3, HALVES * PAIRS):
                squares(n)

        @block.vector
        def _(dve):
            dve.memset(eps_sb[:, :], EPS).then_inc(eps_set, 1)
            dve.wait_ge(const_in, 16)
            dve.tensor_copy(ident_bf[:, :], ident).then_inc(identbf_done, 1)

            def scales(sums, scale, n, length, summed, scaled):
                dve.wait_ge(summed, n)
                dve.tensor_scalar(scale[:, 0, :], sums[:, :], 1.0 / length, EPS, ALU.mult,
                                  ALU.max).then_inc(scaled, 1)
                dve.wait_ge(scaled, 1)
                dve.tensor_scalar(scale[:, 1, :], scale[:, 0, :], 0.5, None, ALU.mult).then_inc(scaled, 1)
                dve.tensor_scalar(scale[:, 2, :], scale[:, 0, :], -0.5, None, ALU.mult).then_inc(scaled, 1)

            def ternary(w, scale, tern, m, cmp, ready):
                dve.wait_ge(cmp, m + 1)
                dve.scalar_tensor_tensor(tern[:, m, :], w[:, m, :], scale[:, 1, m:m + 1], tern[:, m, :],
                                         ALU.is_gt, ALU.subtract).then_inc(ready, 1)

            dve.wait_ge(bias_set, 3)
            dve.tensor_tensor(bias_parts[32:33, :], bias_sb[32:33, :],
                              bias_parts[32:33, :].bitcast(F32), ALU.subtract).then_inc(bias_set, 1)
            dve.wait_ge(slope_in, 16)
            for g in range(GRP):
                dve.scalar_tensor_tensor(alibi[:, g, :], rel, slope_sb[:, g:g + 1], neg, ALU.mult,
                                         ALU.add).then_inc(alibi_done, 1)

            def low_rank_factors():
                dve.wait_ge(rows_in, 32)
                dve.wait_ge(small_in, 16 * SMALL_LOADS)
                dve.reciprocal(fc_scale[:, 3, :], fc_scale[:, 0, :]).then_inc(u_step, 1)
                dve.wait_ge(u_step, 1)
                recip = fc_scale[:, 3, :].rearrange("p (m o) -> p m o", o=1).broadcast_to([P, KH, RANK])
                dve.scalar_tensor_tensor(u_scaled[:, :, :], u_sb[:, :, :], rows_sb[:, R_GATE:R_GATE + 1],
                                         recip, ALU.mult, ALU.mult).then_inc(u_step, 1)
                dve.wait_ge(u_step, 2)
                dve.tensor_copy(u_parts[:, :, 0, :], u_scaled[:, :, :]).then_inc(u_step, 1)
                dve.tensor_copy(u_parts[:, :, 2, :], u_scaled[:, :, :]).then_inc(u_step, 1)
                dve.wait_ge(u_step, 4)
                for part in (1, 3):
                    dve.tensor_tensor(u_parts[:, :, part, :], u_scaled[:, :, :],
                                      u_parts[:, :, part - 1, :].bitcast(F32), ALU.subtract).then_inc(u_step, 1)

            def stats(b, which, hidden_state, src, other, src_done, count, h_sem, bn_sem, var_sem):
                dve.wait_ge(src_done, count)
                dve.tensor_tensor(hidden_state[:, b, :], src, other, ALU.add).then_inc(h_sem, 1)
                dve.wait_ge(h_sem, b + 1)
                dve.bn_stats(bn6[:, which, b, :], hidden_state[:, b, :]).then_inc(bn_sem, 1)
                dve.wait_ge(bn_sem, b + 1)
                dve.bn_aggr(mv[:, which, b, :], bn6[:, which, b, :]).then_inc(var_sem, 1)

            def normalise(f, which, hidden_state, std_sem, rstd_sem, z_sem):
                dve.wait_ge(std_sem, f + 1)
                dve.reciprocal(rstd[:, which, f * BH:(f + 1) * BH],
                               std[:, which, f * BH:(f + 1) * BH]).then_inc(rstd_sem, 1)
                dve.wait_ge(rstd_sem, f + 1)
                for b in range(f * BH, (f + 1) * BH):
                    dve.tensor_scalar(z[:, b, :], hidden_state[:, b, :], mv[:, which, b, 0:1],
                                      rstd[:, which, b:b + 1], ALU.subtract, ALU.mult).then_inc(z_sem, 1)

            def low_part(dst, src, hi, count, hi_ready, signal):
                dve.wait_ge(hi_ready, count)
                dve.tensor_tensor(dst, src, hi.bitcast(F32), ALU.subtract).then_inc(signal, 1)

            def stats1(b):
                stats(b, 0, h1, tok_ps[b], posb[:, :], tok_done, b + 1, h1_ready, bn1, var1)

            def stats2(b):
                stats(b, 1, h2, o_ps[b // BH][:, (b % BH) * E:(b % BH + 1) * E], h1[:, b, :], o_done,
                      b // BH + 1, h2_ready, bn2, var2)

            def zt_low(f):
                low_part(zt_lo[f][:, :, :], zt_ps[f][:, :].rearrange("p (k t) -> p k t", k=KE),
                         zt_hi[f][:, :, :], f + 1, zt_hi_ready, zt_lo_ready)

            def yt_low(f):
                low_part(yt_lo[f][:, :, :], yt_ps[f][:, :].rearrange("p (g t) -> p g t", g=GRP),
                         yt_hi[f][:, :, :], f + 1, yt_hi_ready, yt_lo_ready)

            def z2t_low(f):
                low_part(z2t_lo[f][:, :, :], z2t_ps[f][:, :].rearrange("p (k t) -> p k t", k=KE),
                         z2t_hi[f][:, :, :], f + 1, z2t_hi_ready, z2t_lo_ready)

            def spread(f, half, dst, src, ready, signal):
                dve.wait_ge(ready, f + 1)
                n = slice(half * IPH, (half + 1) * IPH)
                for a in range(SPREAD_DVE):
                    last = dve.tensor_scalar(dst[:, f, :, n, a, :], src[:, f, :, n, :], mask[:, a:a + 1],
                                             None, ALU.mult)
                last.then_inc(signal, 1)

            def left_over(f, ps, part, left, first, signal):
                dve.wait_ge(first, f + 1)
                dve.tensor_tensor(left[:, f, :, :], ps[f][:, :].rearrange("p (n s) -> p n s", s=S),
                                  part[:, f, 0, :, :], ALU.subtract).then_inc(signal, 1)

            def later_parts(f, part, left, left_ready, second, ready):
                dve.wait_ge(left_ready, f + 1)
                dve.tensor_copy(part[:, f, 1, :, :], left[:, f, :, :]).then_inc(second, 1)
                dve.wait_ge(second, f + 1)
                dve.tensor_tensor(part[:, f, 2, :, :], left[:, f, :, :], part[:, f, 1, :, :],
                                  ALU.subtract).then_inc(ready, 1)

            def per_key(t, f):
                return t[:, f, :].rearrange("p (n o) -> p n o", o=1).broadcast_to([P, GRP * IPH, S])

            def softmax_shift(f):
                dve.wait_ge(alibi_done, GRP)
                dve.wait_ge(s_done, GRP * (f + 1))
                for g in range(GRP):
                    ab = alibi[:, g, :].rearrange("p (o s) -> p o s", o=1).broadcast_to([P, IPH, S])
                    src = s_ps[f][:, g * HT:(g + 1) * HT].rearrange("p (i s) -> p i s", s=S)
                    dve.scalar_tensor_tensor(score[:, f, g, :, :], src, float(D) ** -0.5, ab, ALU.mult,
                                             ALU.add).then_inc(score_ready, 1)
                dve.wait_ge(score_ready, GRP * (f + 1))
                rows_ = score[:, f, :, :, :].rearrange("p g i s -> p (g i) s")
                dve.tensor_reduce(smax[:, f, :], rows_, AX.X, ALU.max).then_inc(max_ready, 1)
                dve.wait_ge(max_ready, f + 1)
                dve.tensor_tensor(shifted[:, f, :, :], rows_, per_key(smax, f),
                                  ALU.subtract).then_inc(shift_ready, 1)

            def softmax_norm(f):
                dve.wait_ge(exp_ready, f + 1)
                dve.tensor_reduce(ssum[:, f, :], expd[:, f, :, :], AX.X, ALU.add).then_inc(sum_ready, 1)
                dve.wait_ge(sum_ready, f + 1)
                dve.reciprocal(srec[:, f, :], ssum[:, f, :]).then_inc(rec_ready, 1)
                dve.wait_ge(rec_ready, f + 1)
                dve.tensor_tensor(prob[:, f, :, :].rearrange("p g (i s) -> p (g i) s", s=S),
                                  expd[:, f, :, :], per_key(srec, f), ALU.mult).then_inc(prob_ready, 1)

            def query_parts(f):
                left_over(f, q_ps, q_part, rest, q_first, q_rest)
                later_parts(f, q_part, rest, q_rest, q_second, q_ready)
                left_over(f, k_ps, k_part, rest_k, k_first, k_rest)

            def prob_parts(f):
                left_over(f, pt_ps, p_part, rest, p_first, p_rest)
                later_parts(f, p_part, rest, p_rest, p_second, p_ready)

            dve.wait_ge(posb_done, 1)
            stats1(0)
            stats1(1)
            normalise(0, 0, h1, std1, rstd1, z1_ready)
            stats1(2)
            zt_low(0)
            stats1(3)
            normalise(1, 0, h1, std1, rstd1, z1_ready)
            query_parts(0)
            zt_low(1)
            spread(0, 0, q_spread, q_part, q_ready, q_spread_dve)
            spread(0, 1, q_spread, q_part, q_ready, q_spread_dve)
            scales(fc_sum, fc_scale, KH, E, fc_summed, fc_scaled)
            query_parts(1)
            left_over(0, v_ps, v_part, rest_v, v_first, v_rest)
            spread(1, 0, q_spread, q_part, q_ready, q_spread_dve)
            spread(1, 1, q_spread, q_part, q_ready, q_spread_dve)
            scales(mlp_sum, mlp_scale, KE, HID, mlp_summed, mlp_scaled)
            softmax_shift(0)
            left_over(1, v_ps, v_part, rest_v, v_first, v_rest)
            softmax_norm(0)
            for m in range(KH):
                ternary(fc_sb, fc_scale, fc_tern, m, fc_cmp, fc_ternary)
            softmax_shift(1)
            prob_parts(0)
            spread(0, 0, p_spread, p_part, p_ready, p_spread_dve)
            softmax_norm(1)
            spread(0, 1, p_spread, p_part, p_ready, p_spread_dve)
            low_rank_factors()
            prob_parts(1)
            spread(1, 0, p_spread, p_part, p_ready, p_spread_dve)
            yt_low(0)
            spread(1, 1, p_spread, p_part, p_ready, p_spread_dve)
            for o in range(KE):
                ternary(mlp_sb, mlp_scale, mlp_tern, o, mlp_cmp, mlp_ternary)
            stats2(0)
            stats2(1)
            normalise(0, 1, h2, std2, rstd2, z2_ready)
            z2t_low(0)
            yt_low(1)

            def low_a_copy(f):
                dve.wait_ge(low_a_done, f + 1)
                dve.tensor_copy(low_a[:, f, :], low_ps[f][0:2 * RANK, 0:HT]).then_inc(low_a_ready, 1)

            def low_low(f):
                dve.wait_ge(low_hi_ready, f + 1)
                dve.tensor_tensor(low_t[2 * RANK:4 * RANK, f, :], low_ps[f][2 * RANK:4 * RANK, HT:2 * HT],
                                  low_t[2 * RANK:4 * RANK, f, :].bitcast(F32),
                                  ALU.subtract).then_inc(low_ready, 1)

            def result(f):
                dve.wait_ge(mlp_step, PAIRS * (f + 1))
                dve.wait_ge(h2t_ready, f + 1)
                for m in range(KE):
                    dve.scalar_tensor_tensor(out_sb[:, f, m, :], mlp_ps[f][:, m * HT:(m + 1) * HT],
                                             mlp_scale[:, 0, m:m + 1], h2_t[:, f, m, :], ALU.mult,
                                             ALU.add).then_inc(out_ready, 1)

            def squares(n):
                r = n % RING
                dve.wait_ge(relu_ready, 2 * n + 2)
                if n >= RING:
                    dve.wait_ge(mlp_step, n - RING + 1)
                dve.tensor_tensor(sq[:, r, :, :], relu[:, r, :, :], relu[:, r, :, :],
                                  ALU.mult).then_inc(sq_ready, 1)
                dve.wait_ge(sq_ready, n + 1)
                low_part(sq_lo[:, r, :, :], sq[:, r, :, :], sq_hi[:, r, :, :], n + 1, sq_hi_ready,
                         sq_lo_ready)

            low_a_copy(0)
            low_low(0)
            stats2(2)
            stats2(3)
            normalise(1, 1, h2, std2, rstd2, z2_ready)
            squares(0)
            squares(1)
            z2t_low(1)
            squares(2)
            low_a_copy(1)
            low_low(1)
            for n in range(3, PAIRS + 2):
                squares(n)
            result(0)
            for n in range(PAIRS + 2, HALVES * PAIRS):
                squares(n)
            result(1)

        @block.gpsimd
        def _(pool):
            def split(w, hi, lo, signal):
                pool.tensor_scalar(hi, w, 1.0, 1.0, ALU.mult, ALU.mult).then_inc(signal, 1)
                pool.wait_ge(signal, 1)
                pool.tensor_tensor(lo, w, hi.bitcast(F32), ALU.subtract).then_inc(signal, 1)

            pool.memset(bias_parts[:, :].bitcast(F32), 0.0).then_inc(bias_set, 1)
            pool.memset(ones_f[:, :], 1.0).then_inc(ones_set, 1)
            pool.wait_ge(ones_set, 1)
            pool.tensor_scalar(ones[:, :], ones_f[:, :], 1.0, 1.0, ALU.mult, ALU.mult).then_inc(ones_set, 1)
            pool.wait_ge(rows_in, 32)
            pool.tensor_tensor(posb[:, :], pos_sb[:, :], rows_sb[:, R_TOKB:R_TOKB + E],
                               ALU.add).then_inc(posb_done, 1)
            for which, hi_ready, signal in ((1, q_w_hi, q_split), (0, k_w_hi, k_split),
                                            (2, v_w_hi, v_w_split)):
                c = which * E
                pool.wait_ge(hi_ready, 1)
                pool.tensor_tensor(kqv_lo[:, :, c:c + E], kqv_sb[:, :, c:c + E],
                                   kqv_hi[:, :, c:c + E].bitcast(F32), ALU.subtract).then_inc(signal, 1)
            pool.wait_ge(proj_in, 16)
            split(proj_sb[:, :, :], proj_hi[:, :, :], proj_lo[:, :, :], proj_split)
            def later_parts(f, part, left, left_ready, second, ready):
                pool.wait_ge(left_ready, f + 1)
                pool.tensor_scalar(part[:, f, 1, :, :], left[:, f, :, :], 1.0, 1.0, ALU.mult,
                                   ALU.mult).then_inc(second, 1)
                pool.wait_ge(second, f + 1)
                pool.tensor_tensor(part[:, f, 2, :, :], left[:, f, :, :], part[:, f, 1, :, :],
                                   ALU.subtract).then_inc(ready, 1)

            def below(w, scale, dst, tiles, scaled, signal):
                pool.wait_ge(scaled, 3)
                for m in tiles:
                    pool.tensor_scalar(dst[:, m, :], w[:, m, :], scale[:, 2, m:m + 1], None,
                                       ALU.is_lt).then_inc(signal, 1)

            pool.wait_ge(small_in, 16 * SMALL_LOADS)
            split(v_sb[:, :, :], v_parts[:, :, 0, :], v_parts[:, :, 1, :], v_split)
            later_parts(0, k_part, rest_k, k_rest, k_second, k_ready)
            later_parts(1, k_part, rest_k, k_rest, k_second, k_ready)
            below(fc_sb, fc_scale, fc_tern, range(KH), fc_scaled, fc_cmp)
            later_parts(0, v_part, rest_v, v_rest, v_second, v_ready)
            later_parts(1, v_part, rest_v, v_rest, v_second, v_ready)
            below(mlp_sb, mlp_scale, mlp_tern, range(KE), mlp_scaled, mlp_cmp)


def shape_constants():
    p = np.arange(P)
    key, query = np.arange(S)[None, :], (p % S)[:, None]
    c = np.zeros((P, C_END), np.float32)
    c[:, C_ID:C_ID + P] = np.eye(P)
    c[:, C_MASK:C_MASK + 8] = p[:, None] // 16 == np.arange(8)[None, :]
    c[:, C_REL:C_REL + S] = np.where(key <= query, key - query, 0)
    c[:, C_NEG:C_NEG + S] = np.where(key > query, NEG_INF, 0.0)
    return c


def kernel(x, L0_tok_W, L0_tok_b, L0_tok_pos_emb, L0_attn_W_kqv, L0_attn_b_kqv, L0_attn_W_proj,
           L0_attn_b_proj, L0_attn_slopes, L0_ffn_fast_b, L0_ffn_w_fc, L0_ffn_w_proj, L0_ffn_u,
           L0_ffn_v, L0_ffn_gate):
    import concourse.bacc as bacc
    from concourse.bass_utils import run_bass_kernel_spmd

    a = np.asarray
    patches = a(x).reshape(IMAGES, CH, SIDE, PATCH, SIDE, PATCH).transpose(1, 3, 5, 0, 2, 4)
    arrays = {
        "x_t": patches.reshape(FEAT, TOK),
        "wtok_t": a(L0_tok_W).T,
        "consts": shape_constants(),
        "rows": np.concatenate([a(L0_tok_b), a(L0_ffn_gate).reshape(1)]).reshape(1, R_END),
        "pos": np.tile(a(L0_tok_pos_emb), (IPB, 1)),
        "w_kqv": a(L0_attn_W_kqv),
        "bias_row": np.concatenate([a(L0_attn_b_kqv), a(L0_attn_b_proj)]).reshape(1, 4 * E),
        "slopes": np.repeat(a(L0_attn_slopes).reshape(GRP, HPG), S, axis=1).T,
        "w_proj": a(L0_attn_W_proj),
        "w_fc": a(L0_ffn_w_fc),
        "w_mlp": a(L0_ffn_w_proj),
        "u_nat": a(L0_ffn_u),
        "v_t": a(L0_ffn_v).T,
        "fb_t": a(L0_ffn_fast_b).T,
    }
    arrays = {n: np.ascontiguousarray(t) for n, t in arrays.items()}
    nc = bacc.Bacc("TRN2", target_bir_lowering=False, num_devices=1)
    args = {n: nc.dram_tensor(n, t.shape, mybir.dt.from_np(t.dtype), kind="ExternalInput").ap()
            for n, t in arrays.items()}
    out_t = nc.dram_tensor("out_t", (E, TOK), F32, kind="ExternalOutput").ap()
    build_program(nc, out_t=out_t, **args)
    got = run_bass_kernel_spmd(nc, [arrays], core_ids=[0])
    return a(got.results[0]["out_t"]).T.reshape(IMAGES, S, E)
```

```python
from contextlib import ExitStack

import numpy as np

import concourse.bass as bass
from concourse import mybir

F32 = mybir.dt.float32
F32R = mybir.dt.float32r
BF16 = mybir.dt.bfloat16
ALU = mybir.AluOpType
ACT = mybir.ActivationFunctionType
AX = mybir.AxisListType

P = 128
IMAGES, CH, IMG, PATCH = 32, 3, 64, 16
SIDE = IMG // PATCH
S = SIDE * SIDE
TOK = IMAGES * S
FEAT = CH * PATCH * PATCH
E = 256
H, D = 16, 16
HID, RANK = 1024, 16
KF, KE, KH = FEAT // P, E // P, HID // P
HALVES = 2
HT = TOK // HALVES
BH = HT // P
BLOCKS = TOK // P
IPB = P // S
HPG = P // D
GRP = H // HPG
IPH = IMAGES // HALVES
NEG_INF = -1e30
EPS = 1e-5
SPREAD_DVE, SPREAD_ACT = 5, 2

C_ID, C_MASK, C_REL, C_NEG = 0, P, P + 8, P + 8 + S
C_END = C_NEG + S
R_TOKB, R_GATE = 0, E
R_END = E + 1
VW = D + 2
ALL, FIRST, SECOND = slice(0, GRP * IPH), slice(0, IPH), slice(IPH, GRP * IPH)
PARTS = 3


def build_program(nc, x_t, wtok_t, consts, rows, pos, w_kqv, bias_row, slopes, w_proj, proj_bias,
                  w_fc, w_mlp, u_nat, v_t, fb_t, out_t):
    with ExitStack() as ctx:
        def sb(name, shape, dt=F32):
            return ctx.enter_context(nc.sbuf_tensor(name, shape, dt))

        def sem(name):
            return ctx.enter_context(nc.semaphore(name))

        bank = [ctx.enter_context(nc.psum_tensor(f"bank{i}", [P, 512], F32)) for i in range(8)]

        x_sb = sb("x_sb", [P, KF, TOK])
        wtok_sb = sb("wtok_sb", [P, KF, E])
        const_sb = sb("const_sb", [P, C_END])
        rows_sb = sb("rows_sb", [P, R_END])
        pos_sb = sb("pos_sb", [P, E])
        kqv_sb = sb("kqv_sb", [P, KE, 3 * E])
        bias_sb = sb("bias_sb", [64, 3 * E])
        slope_sb = sb("slope_sb", [P, GRP])
        proj_sb = sb("proj_sb", [P, KE, E])
        proj_bias_sb = sb("proj_bias_sb", [P, E])
        fc_sb = sb("fc_sb", [P, KH, E])
        mlp_sb = sb("mlp_sb", [P, KE, HID])
        u_sb = sb("u_sb", [P, KH, RANK])
        v_sb = sb("v_sb", [P, KE, RANK])
        fb_sb = sb("fb_sb", [2 * RANK, 4 * RANK])

        ident = const_sb[:, C_ID:C_ID + P]
        mask = const_sb[:, C_MASK:C_MASK + 8]
        rel = const_sb[:, C_REL:C_REL + S]
        neg = const_sb[:, C_NEG:C_NEG + S]

        ident_bf = sb("ident_bf", [P, P], BF16)
        posb = pos_sb
        ident_r = sb("ident_r", [P, P], F32R)
        alibi = sb("alibi", [P, GRP, S])
        alibi_hi = sb("alibi_hi", [P, GRP, S], F32R)
        alibi_lo = sb("alibi_lo", [P, GRP, S], F32R)
        warm = sb("warm", [P, HT], BF16)
        bias_parts = sb("bias_parts", [64, 3 * E], F32R)
        ones_f = sb("ones_f", [64, HT])
        ones = sb("ones", [64, HT], F32R)
        kqv_hi = sb("kqv_hi", [P, KE, 3 * E], F32R)
        kqv_lo = sb("kqv_lo", [P, KE, 3 * E], F32R)
        proj_hi = sb("proj_hi", [P, KE, E], F32R)
        proj_lo = sb("proj_lo", [P, KE, E], F32R)
        v_parts = sb("v_parts", [P, KE, 2, RANK], F32R)
        fc_sum = sb("fc_sum", [P, KH])
        mlp_sum = sb("mlp_sum", [P, KE])
        fc_scale = sb("fc_scale", [P, 4, KH])
        mlp_scale = sb("mlp_scale", [P, 3, KE])
        fc_tern = sb("fc_tern", [P, KH, E], BF16)
        mlp_tern = sb("mlp_tern", [P, KE, HID], BF16)
        fc_t = sb("fc_t", [P, KE, HID], F32R)
        mlp_t = sb("mlp_t", [P, KH, E], F32R)
        u_scaled = sb("u_scaled", [P, KH, RANK])
        u_parts = sb("u_parts", [P, KH, 4, RANK], F32R)
        u_t = sb("u_t", [4 * RANK, HID], F32R)
        eps_sb = sb("eps_sb", [P, 1])
        table_junk = sb("table_junk", [P, 1])

        h1 = sb("h1", [P, BLOCKS, E])
        h2 = h1
        bn6 = sb("bn6", [P, 2, BLOCKS, 6])
        mv = sb("mv", [P, 2, BLOCKS, 2])
        std = sb("std", [P, 2, BLOCKS])
        rstd = sb("rstd", [P, 2, BLOCKS])
        z = sb("z", [P, BLOCKS, E])
        zt_hi = [sb(f"zt_hi{f}", [P, KE, HT], F32R) for f in range(HALVES)]
        zt_lo = [sb(f"zt_lo{f}", [P, KE, HT], F32R) for f in range(HALVES)]
        q_part = sb("q_part", [P, HALVES, PARTS, GRP * IPH, S], BF16)
        k_part = sb("k_part", [P, HALVES, PARTS, GRP * IPH, S], BF16)
        v_part = sb("v_part", [P, HALVES, PARTS, BH * H, VW], BF16)
        p_part = sb("p_part", [P, HALVES, PARTS, BH * H, S], BF16)
        q_spread = sb("q_spread", [P, HALVES, PARTS, GRP * IPH, HPG, S], BF16)
        p_spread = q_spread
        abs_junk = p_part[:, 0, 0, 0:E // S, :].rearrange("p n s -> p (n s)")
        mlp_junk = mlp_tern[:, 0, :]
        smax = sb("smax", [P, HALVES, GRP * IPH])
        srec = sb("srec", [P, HALVES, BH, H])

        def reuse(base, lot):
            flat = base[:, :, :].rearrange("p k n -> p (k n)")
            return flat[:, lot * HALVES * 2 * HT:(lot + 1) * HALVES * 2 * HT]

        y_tok = reuse(x_sb, 0).rearrange("p (f b e) -> p f b e", f=HALVES, b=BH)
        shifted = reuse(x_sb, 1).rearrange("p (f n s) -> p f n s", f=HALVES, s=S)
        prob = reuse(x_sb, 2).rearrange("p (f g n) -> p f g n", f=HALVES, g=GRP)
        rest = reuse(wtok_sb, 0).rearrange("p (f n s) -> p f n s", f=HALVES, s=S)
        h2_t = reuse(mlp_sb, 1).rearrange("p (f k t) -> p f k t", f=HALVES, k=KE)
        yt_hi, yt_lo, z2t_hi, z2t_lo = zt_hi, zt_lo, zt_hi, zt_lo
        low_a = y_tok[0:2 * RANK, :, 0, :]
        low_t = sb("low_t", [4 * RANK, HALVES, HT], F32R)
        RING = 3
        relu = wtok_sb[:, :, :].rearrange("p (r a) t -> p r a t", a=2)
        sq = kqv_sb[:, :, :].rearrange("p k n -> p (k n)").rearrange("p (r a t) -> p r a t", r=RING, a=2)
        sq_hi = sb("sq_hi", [P, RING, 2, HT], F32R)
        sq_lo = sb("sq_lo", [P, RING, 2, HT], F32R)
        out_sb = reuse(x_sb, 0).rearrange("p (f k t) -> p f k t", f=HALVES, k=KE)
        rest_k = reuse(x_sb, 2).rearrange("p (f n s) -> p f n s", f=HALVES, s=S)
        rest_v = reuse(kqv_sb, 0).rearrange("p (f n s) -> p f n s", f=HALVES, s=S)

        tok_ps = [bank[b][:, 0:E] for b in range(BLOCKS)]
        zt_ps = [bank[4], bank[5]]
        q_ps = [bank[6], bank[1]]
        k_ps = [bank[7], bank[2]]
        v_ps = [bank[0], bank[3]]
        s_ps = [bank[4], bank[5]]
        pt_ps = [bank[6], bank[7]]
        y_ps = [[bank[0], bank[1]], [bank[4], bank[5]]]
        fct_ps = [bank[2 + k][:, :].bitcast(BF16) for k in range(KE)]
        mlpt_ps = [bank[2 + i][:, :].bitcast(BF16) for i in range(2)]
        ut_ps = [bank[2 + i][0:4 * RANK, :] for i in range(2)]
        yt_ps = [bank[6], bank[0]]
        o_ps = [bank[7][:, 0:E], bank[6][:, 0:E], bank[1][:, 0:E], bank[0][:, 0:E]]
        z2t_ps = [bank[6], bank[4]]
        h2t_ps = [bank[5], bank[0]]
        low_ps = [bank[7], bank[1]]
        FCB = [bank[2], bank[3], bank[6], bank[7]]
        mlp_ps = [[bank[5][:, m * HT:(m + 1) * HT] for m in range(KE)],
                  [bank[4][:, 0:HT], bank[0][:, 0:HT]]]

        tok_in = [sem(f"tok_in{i}") for i in range(4)]
        x2_in = [sem(f"x2_in{i}") for i in range(2)]
        const_in = sem("const_in")
        rows_in = sem("rows_in")
        q_in, k_in, v_in = sem("q_in"), sem("k_in"), sem("v_in")
        slope_in = sem("slope_in")
        bias_in = sem("bias_in")
        small_in = sem("small_in")
        proj_in = sem("proj_in")
        proj_bias_in = sem("proj_bias_in")
        residual_ready = sem("residual_ready")
        fc_in = sem("fc_in")
        mlp_in = sem("mlp_in")
        out_done = sem("out_done")
        eps_set = sem("eps_set")
        identbf_done = sem("identbf_done")
        posb_done = sem("posb_done")
        alibi_done = sem("alibi_done")
        alibi_hi_done = sem("alibi_hi_done")
        alibi_ready = sem("alibi_ready")
        identr_done = sem("identr_done")
        warm_set = sem("warm_set")
        v_ones_set = sem("v_ones_set")
        q_w_hi, k_w_hi, v_w_hi = sem("q_w_hi"), sem("k_w_hi"), sem("v_w_hi")
        q_split, k_split, v_w_split = sem("q_split"), sem("k_split"), sem("v_w_split")
        proj_split = sem("proj_split")
        v_split = sem("v_split")
        fc_summed = sem("fc_summed")
        mlp_summed = sem("mlp_summed")
        fc_scaled = sem("fc_scaled")
        mlp_scaled = sem("mlp_scaled")
        fc_cmp = sem("fc_cmp")
        fc_ternary = sem("fc_ternary")
        mlp_cmp = sem("mlp_cmp")
        mlp_ternary = sem("mlp_ternary")
        fct_turned = sem("fct_turned")
        fct_ready = sem("fct_ready")
        mlpt_turned = sem("mlpt_turned")
        mlpt_ready = sem("mlpt_ready")
        u_step = sem("u_step")
        ut_turned = sem("ut_turned")
        ut_ready = sem("ut_ready")
        tok_done = sem("tok_done")
        h1_ready = sem("h1_ready")
        bias_set = sem("bias_set")
        ones_set = sem("ones_set")
        bn1 = sem("bn1")
        var1 = sem("var1")
        std1 = sem("std1")
        rstd1 = sem("rstd1")
        z1_ready = sem("z1_ready")
        zt_turned = sem("zt_turned")
        zt_hi_ready = sem("zt_hi_ready")
        zt_lo_ready = sem("zt_lo_ready")
        q_done = sem("q_done")
        k_done = sem("k_done")
        v_done = sem("v_done")
        q_first, q_rest, q_second, q_ready = (sem(f"q_{n}") for n in ("first", "rest", "second", "ready"))
        k_first, k_rest, k_second, k_ready = (sem(f"k_{n}") for n in ("first", "rest", "second", "ready"))
        v_first, v_rest, v_second, v_ready = (sem(f"v_{n}") for n in ("first", "rest", "second", "ready"))
        p_first, p_rest, p_second, p_ready = (sem(f"p_{n}") for n in ("first", "rest", "second", "ready"))
        q_spread_dve = sem("q_spread_dve")
        q_spread_act = sem("q_spread_act")
        q_spread_pool = sem("q_spread_pool")
        s_done = sem("s_done")
        max_ready = sem("max_ready")
        shift_ready = sem("shift_ready")
        prob_ready = sem("prob_ready")
        norm_ready = sem("norm_ready")
        pt_turned = sem("pt_turned")
        p_spread_dve = sem("p_spread_dve")
        p_spread_act = sem("p_spread_act")
        p_spread_pool = sem("p_spread_pool")
        y_done = sem("y_done")
        y_ready = sem("y_ready")
        yt_turned = sem("yt_turned")
        yt_hi_ready = sem("yt_hi_ready")
        yt_lo_ready = sem("yt_lo_ready")
        o_done = sem("o_done")
        h2_ready = sem("h2_ready")
        bn2 = sem("bn2")
        var2 = sem("var2")
        std2 = sem("std2")
        rstd2 = sem("rstd2")
        z2_ready = sem("z2_ready")
        z2t_turned = sem("z2t_turned")
        h2t_turned = sem("h2t_turned")
        h2t_ready = sem("h2t_ready")
        z2t_hi_ready = sem("z2t_hi_ready")
        z2t_lo_ready = sem("z2t_lo_ready")
        low_a_done = sem("low_a_done")
        low_a_ready = sem("low_a_ready")
        low_c_done = sem("low_c_done")
        low_hi_ready = sem("low_hi_ready")
        low_ready = sem("low_ready")
        fc_done = sem("fc_done")
        relu_ready = sem("relu_ready")
        sq_ready = sem("sq_ready")
        sq_hi_ready = sem("sq_hi_ready")
        sq_lo_ready = sem("sq_lo_ready")
        mlp_step = sem("mlp_step")
        mlp_tile = sem("mlp_tile")
        out_ready = sem("out_ready")

        block = ctx.enter_context(nc.Block())
        SMALL_LOADS = 4
        WARM_PRODUCTS = 16
        CHUNKS = ((0, 1), (1, 1), (2, 2), (4, 2))
        PAIRS = KH // 2

        @block.sync
        def _(sp):
            for i, (k, n) in enumerate(CHUNKS):
                rows_ = slice(k * P, (k + n) * P)
                sp.dma_start(x_sb[:, k:k + n, 0:HT],
                             x_t[rows_, 0:HT].rearrange("(k p) t -> p k t", p=P)).then_inc(tok_in[i], 16)
                sp.dma_start(wtok_sb[:, k:k + n, :],
                             wtok_t[rows_, :].rearrange("(k p) e -> p k e", p=P)).then_inc(tok_in[i], 16)
            half = KF // 2
            for i in range(2):
                sp.dma_start(x_sb[:, i * half:(i + 1) * half, HT:TOK],
                             x_t[i * half * P:(i + 1) * half * P, HT:TOK].rearrange("(k p) t -> p k t", p=P)
                             ).then_inc(x2_in[i], 16)
            def load_kqv(which, signal):
                c = which * E
                sp.dma_start(kqv_sb[:, :, c:c + E], w_kqv[:, c:c + E].rearrange("(k p) n -> p k n", p=P)
                             ).then_inc(signal, 16)

            load_kqv(1, q_in)
            sp.dma_start(fc_sb[:, :, :], w_fc.rearrange("(m p) e -> p m e", p=P)).then_inc(fc_in, 16)
            load_kqv(0, k_in)
            load_kqv(2, v_in)
            sp.dma_start(proj_sb[:, :, :], w_proj.rearrange("(k p) n -> p k n", p=P)).then_inc(proj_in, 16)
            sp.dma_start(proj_bias_sb[:, :], proj_bias.broadcast_to([P, E])).then_inc(proj_bias_in, 16)
            sp.dma_start(mlp_sb[:, :, :], w_mlp.rearrange("(k p) n -> p k n", p=P)).then_inc(mlp_in, 16)
            sp.dma_start(u_sb[:, :, :], u_nat.rearrange("(m p) r -> p m r", p=P)).then_inc(small_in, 16)
            sp.dma_start(v_sb[:, :, :], v_t.rearrange("(k p) r -> p k r", p=P)).then_inc(small_in, 16)
            for i in range(2):
                sp.dma_start(fb_sb[i * RANK:(i + 1) * RANK, :].rearrange("p (a r) -> p a r", a=4),
                             fb_t.rearrange("p (o r) -> p o r", o=1).broadcast_to([RANK, 4, RANK])
                             ).then_inc(small_in, 16)
            for f in range(HALVES):
                for m in range(KE):
                    sp.wait_ge(out_ready, f * KE + m + 1)
                    sp.dma_start(out_t[m * P:(m + 1) * P, f * HT:(f + 1) * HT],
                                 out_sb[:, f, m, :]).then_inc(out_done, 16)
            sp.wait_ge(out_done, 16 * HALVES * KE)

        @block.tensor
        def _(pe):
            def split_product(out, pairs):
                for i, (lhs, rhs) in enumerate(pairs):
                    mm = pe.matmul(out, lhs, rhs, start=i == 0, stop=i == len(pairs) - 1)
                return mm

            def embed(k, b):
                return pe.matmul(tok_ps[b], x_sb[:, k, b * P:(b + 1) * P], wtok_sb[:, k, :],
                                 start=k == 0, stop=k == KF - 1)

            def turn_z(f, src, dst, ready, signal):
                for b in range(BH):
                    pe.wait_ge(ready, f * BH + b + 1)
                    for k in range(KE):
                        mm = pe.transpose(dst[:, k * HT + b * P:k * HT + (b + 1) * P],
                                          src(f * BH + b)[:, k * P:(k + 1) * P], ident)
                mm.then_inc(signal, 1)

            def query_key(f, which, ps, weights, signal):
                pe.wait_ge(weights, 1)
                pe.wait_ge(bias_set, 4)
                pe.wait_ge(ones_set, 2)
                pe.wait_ge(zt_hi_ready, f + 1)
                pe.wait_ge(zt_lo_ready, f + 1)
                for g in range(GRP):
                    c = which * E + g * P
                    pairs = [(bias_parts[:, c:c + P], ones[:, :])]
                    for k in range(KE):
                        hi, lo = kqv_hi[:, k, c:c + P], kqv_lo[:, k, c:c + P]
                        pairs += [(hi, zt_hi[f][:, k, :]), (hi, zt_lo[f][:, k, :]),
                                  (lo, zt_hi[f][:, k, :])]
                    mm = split_product(ps[f][:, g * HT:(g + 1) * HT], pairs)
                mm.then_inc(signal, 1)

            def value_product(f):
                pe.wait_ge(v_w_split, 1)
                for b in range(BH):
                    pairs = [(ones[:, 0:P], bias_parts[:, 2 * E:3 * E])]
                    for k in range(KE):
                        zh, zl = (t[f][:, k, b * P:(b + 1) * P] for t in (zt_hi, zt_lo))
                        wh, wl = (t[:, k, 2 * E:3 * E] for t in (kqv_hi, kqv_lo))
                        pairs += [(zh, wh), (zh, wl), (zl, wh)]
                    mm = split_product(v_ps[f][:, b * E:(b + 1) * E], pairs)
                mm.then_inc(v_done, 1)

            def bf16_product(out, lhs, rhs, fresh=True):
                order = [(i, n - i) for n in range(PARTS - 1, -1, -1) for i in range(n + 1)]
                for n, (i, j) in enumerate(order):
                    mm = pe.matmul(out, lhs(i), rhs(j), start=fresh and n == 0, stop=n == len(order) - 1,
                                   skip_group_check=not fresh)
                return mm

            def score_bias(f):
                pe.wait_ge(alibi_ready, 1)
                pe.wait_ge(identr_done, 1)
                for g in range(GRP):
                    for i, part in enumerate((alibi_hi, alibi_lo)):
                        bias = part[:, g, :].rearrange("p (o s) -> p o s", o=1).broadcast_to([P, IPH, S])
                        pe.matmul(s_ps[f][:, g * HT:(g + 1) * HT], ident_r[:, :], bias,
                                  start=g == 0 and i == 0, stop=False, skip_group_check=True)

            def scores(f, g):
                pe.wait_ge(k_ready, f + 1)
                for spread_by in (q_spread_dve, q_spread_act, q_spread_pool):
                    pe.wait_ge(spread_by, f + 1)
                for gi in range(g * IPH, (g + 1) * IPH):
                    mm = bf16_product(s_ps[f][:, gi * S:(gi + 1) * S],
                                      lambda i: q_spread[:, f, i, gi, :, :],
                                      lambda j: k_part[:, f, j, gi, :], fresh=False)
                mm.then_inc(s_done, 1)

            def turn_probs(f):
                pe.wait_ge(prob_ready, f + 1)
                for b in range(BH):
                    for g in range(GRP):
                        c = (b * GRP + g) * P
                        mm = pe.transpose(pt_ps[f][:, c:c + P], prob[:, f, g, b * P:(b + 1) * P], ident)
                mm.then_inc(pt_turned, 1)

            def values(f, b, heads=range(H)):
                pe.wait_ge(v_ready, f + 1)
                pe.wait_ge(v_ones_set, PARTS)
                for spread_by in (p_spread_dve, p_spread_act, p_spread_pool):
                    pe.wait_ge(spread_by, BH * f + b + 1)
                for h in heads:
                    bh = b * H + h
                    mm = bf16_product(y_ps[f][b][:, h * (D + 1):(h + 1) * (D + 1)],
                                      lambda i: p_spread[:, f, i, bh, :, :],
                                      lambda j: v_part[:, f, j, bh, 0:D + 1])
                if h == H - 1:
                    mm.then_inc(y_done, 1)

            def turn_y(f):
                pe.wait_ge(y_ready, BH * (f + 1))
                for b in range(BH):
                    for g in range(GRP):
                        c = g * HT + b * P
                        mm = pe.transpose(yt_ps[f][:, c:c + P], y_tok[:, f, b, g * P:(g + 1) * P], ident)
                mm.then_inc(yt_turned, 1)

            def project(f, blocks=range(BH)):
                pe.wait_ge(proj_split, 2)
                pe.wait_ge(yt_hi_ready, f + 1)
                pe.wait_ge(yt_lo_ready, f + 1)
                for b in blocks:
                    pairs = []
                    for g in range(GRP):
                        yh, yl = (t[f][:, g, b * P:(b + 1) * P] for t in (yt_hi, yt_lo))
                        pairs += [(yh, proj_hi[:, g, :]), (yh, proj_lo[:, g, :]), (yl, proj_hi[:, g, :])]
                    split_product(o_ps[f * BH + b], pairs).then_inc(o_done, 1)

            def low_rank_a(f):
                pe.wait_ge(v_split, 2)
                pe.wait_ge(z2t_hi_ready, f + 1)
                pe.wait_ge(z2t_lo_ready, f + 1)
                pairs = []
                for k in range(KE):
                    vp = v_parts[:, k, :, :]
                    pairs += [(vp, z2t_hi[f][:, k, :]), (vp, z2t_lo[f][:, k, :])]
                split_product(low_ps[f][0:2 * RANK, 0:HT], pairs).then_inc(low_a_done, 1)

            def low_rank_c(f):
                pe.wait_ge(low_a_ready, f + 1)
                pe.wait_ge(small_in, 16 * SMALL_LOADS)
                pe.matmul(low_ps[f][0:4 * RANK, HT:2 * HT], fb_sb[:, :], low_a[:, f, :],
                          start=True, stop=True).then_inc(low_c_done, 1)

            def hidden_main(f, j):
                n = f * PAIRS + j
                if n >= len(FCB):
                    pe.wait_ge(relu_ready, 2 * (n - len(FCB) + 1))
                for a in range(2):
                    m = 2 * j + a
                    for k in range(KE):
                        w = fc_t[:, k, m * P:(m + 1) * P]
                        for i, part in enumerate((z2t_hi, z2t_lo)):
                            pe.matmul(FCB[n % len(FCB)][:, a * HT:(a + 1) * HT], w, part[f][:, k, :],
                                      start=a == 0 and k == 0 and i == 0, stop=False,
                                      skip_group_check=True)

            def hidden_low(f, j):
                pe.wait_ge(low_ready, f + 1)
                n = f * PAIRS + j
                for a in range(2):
                    m = 2 * j + a
                    mm = pe.matmul(FCB[n % len(FCB)][:, a * HT:(a + 1) * HT], u_t[:, m * P:(m + 1) * P],
                                   low_t[:, f, :], start=False, stop=True, skip_group_check=True)
                mm.then_inc(fc_done, 1)

            def hidden(f, j):
                hidden_main(f, j)
                hidden_low(f, j)

            def mlp_out(f, j):
                n = f * PAIRS + j
                pe.wait_ge(sq_hi_ready, n + 1)
                pe.wait_ge(sq_lo_ready, n + 1)
                last = j == PAIRS - 1
                order = [(a, m) for m in range(KE) for a in range(2)] if last else \
                    [(a, m) for a in range(2) for m in range(KE)]
                for a, m in order:
                    w = mlp_t[:, 2 * j + a, m * P:(m + 1) * P]
                    for i, part in enumerate((sq_hi, sq_lo)):
                        mm = pe.matmul(mlp_ps[f][m], w, part[:, n % RING, a, :],
                                       start=j == 0 and a == 0 and i == 0 and (m == 0 or f == 1),
                                       stop=last and a == 1 and i == 1, skip_group_check=True)
                    if last and a == 1 and m == 0:
                        mm.then_inc(mlp_tile, 1)
                mm.then_inc(mlp_step, 1)

            def turn_fc():
                pe.wait_ge(identbf_done, 1)
                pe.wait_ge(fc_ternary, KH)
                for k in range(KE):
                    pe.wait_ge(ut_ready, k + 1)
                    for m in range(KH):
                        mm = pe.transpose(fct_ps[k][:, m * P:(m + 1) * P],
                                          fc_tern[:, m, k * P:(k + 1) * P], ident_bf[:, :])
                    mm.then_inc(fct_turned, 1)

            def turn_mlp():
                pe.wait_ge(mlp_ternary, KE)
                for i in range(2):
                    pe.wait_ge(fct_ready, i + 1)
                    for m in range(4):
                        for o in range(KE):
                            c = (m * KE + o) * P
                            mm = pe.transpose(mlpt_ps[i][:, c:c + P],
                                              mlp_tern[:, o, (4 * i + m) * P:(4 * i + m + 1) * P],
                                              ident_bf[:, :])
                    mm.then_inc(mlpt_turned, 1)

            def turn_u():
                pe.wait_ge(u_step, 6)
                for i in range(2):
                    for m in range(4):
                        mm = pe.transpose(ut_ps[i][:, m * P:(m + 1) * P],
                                          u_parts[:, 4 * i + m, :, :].bitcast(F32), ident)
                    mm.then_inc(ut_turned, 1)

            pe.wait_ge(warm_set, 1)
            for _ in range(WARM_PRODUCTS):
                pe.matmul(bank[7][:, 0:HT], warm[:, 0:P], warm[:, :], start=True, stop=True)
            for i, (first, n) in enumerate(CHUNKS):
                pe.wait_ge(tok_in[i], 32)
                for b in range(BH):
                    for k in range(first, first + n):
                        mm = embed(k, b)
                    if first + n == KF:
                        mm.then_inc(tok_done, 1)
            for k in range(KF):
                if k % (KF // 2) == 0:
                    pe.wait_ge(x2_in[k // (KF // 2)], 16)
                mm = embed(k, 2)
            mm.then_inc(tok_done, 1)
            for k in range(2):
                embed(k, 3)
            pe.wait_ge(const_in, 16)
            turn_z(0, lambda b: z[:, b, :], zt_ps[0], z1_ready, zt_turned)
            for k in range(2, KF):
                mm = embed(k, 3)
            mm.then_inc(tok_done, 1)

            query_key(0, 1, q_ps, q_split, q_done)
            query_key(0, 0, k_ps, k_split, k_done)
            turn_z(1, lambda b: z[:, b, :], zt_ps[1], z1_ready, zt_turned)
            pe.wait_ge(h1_ready, BLOCKS)
            value_product(0)
            query_key(1, 1, q_ps, q_split, q_done)
            query_key(1, 0, k_ps, k_split, k_done)
            value_product(1)
            score_bias(0)
            score_bias(1)
            for g in range(GRP):
                scores(0, g)
            scores(1, 0)
            turn_probs(0)
            scores(1, 1)
            pe.wait_ge(k_rest, 2)
            pe.wait_ge(v_rest, 2)
            turn_u()
            values(0, 0, range(0, H // 2))
            turn_probs(1)
            values(0, 0, range(H // 2, H))
            values(0, 1)
            values(1, 0)
            turn_y(0)
            values(1, 1)
            turn_fc()
            pe.wait_ge(p_rest, 2)
            project(0)
            turn_y(1)
            turn_mlp()
            project(1, range(0, 1))

            def turn_z2(f):
                turn_z(f, lambda b: z[:, b, :], z2t_ps[f], z2_ready, z2t_turned)

            def turn_h2(f):
                turn_z(f, lambda b: h2[:, b, :], h2t_ps[f], h2_ready, h2t_turned)

            turn_z2(0)
            project(1, range(1, BH))
            turn_h2(0)
            low_rank_a(0)
            pe.wait_ge(fct_ready, KE)
            pe.wait_ge(mlpt_ready, 2)
            hidden_main(0, 0)
            low_rank_c(0)
            hidden_main(0, 1)
            hidden_low(0, 0)
            hidden_low(0, 1)
            turn_z2(1)
            hidden(0, 2)
            hidden(0, 3)
            pe.wait_ge(h2t_ready, 1)
            mlp_out(0, 0)
            low_rank_a(1)
            turn_h2(1)
            hidden_main(1, 0)
            low_rank_c(1)
            mlp_out(0, 1)
            hidden_low(1, 0)
            hidden(1, 1)
            mlp_out(0, 2)
            hidden(1, 2)
            mlp_out(0, 3)
            hidden(1, 3)
            pe.wait_ge(h2t_ready, 2)
            mlp_out(1, 0)
            mlp_out(1, 1)
            mlp_out(1, 2)
            mlp_out(1, 3)

        @block.scalar
        def _(act):
            for r in (0, 32):
                act.dma_start(bias_sb[r:r + 1, :], bias_row).then_inc(bias_in, 16)
            act.wait_ge(eps_set, 1)
            nc.scalar.activation(table_junk[:, :], eps_sb[:, :], ACT.Sqrt)
            act.wait_ge(bias_in, 32)
            act.wait_ge(bias_set, 1)
            for r in (32, 0):
                nc.scalar.activation(bias_parts[r:r + 1, :], bias_sb[r:r + 1, :],
                                     ACT.Copy).then_inc(bias_set, 1)
                if r == 32:
                    act.wait_ge(tok_in[1], 32)
                    act.dma_start(rows_sb[:, :], rows.broadcast_to([P, R_END])).then_inc(rows_in, 16)
                    act.dma_start(pos_sb[:, :], pos).then_inc(rows_in, 16)
                    act.dma_start(const_sb[:, :], consts).then_inc(const_in, 16)
                    act.dma_start(slope_sb[:, :], slopes).then_inc(slope_in, 16)

            def weight_high(which, arrived, ready):
                act.wait_ge(arrived, 16)
                c = which * E
                nc.scalar.activation(kqv_hi[:, :, c:c + E], kqv_sb[:, :, c:c + E],
                                     ACT.Copy).then_inc(ready, 1)

            def fc_sums(tiles):
                act.wait_ge(fc_in, 16)
                for m in tiles:
                    nc.scalar.activation(abs_junk, fc_sb[:, m, :], ACT.Abs,
                                         accum_out=fc_sum[:, m:m + 1]).then_inc(fc_summed, 1)
                    act.wait_ge(fc_summed, m + 1)

            def norm_std(which, var_ready, std_ready, f):
                act.wait_ge(var_ready, BH * (f + 1))
                nc.scalar.activation(std[:, which, f * BH:(f + 1) * BH],
                                     mv[:, which, f * BH:(f + 1) * BH, 1], ACT.Sqrt,
                                     bias=eps_sb[:, 0:1]).then_inc(std_ready, 1)

            def copy_out(dst, src, turned, count, ready):
                act.wait_ge(turned, count)
                nc.scalar.activation(dst, src, ACT.Copy).then_inc(ready, 1)

            weight_high(1, q_in, q_w_hi)
            norm_std(0, var1, std1, 0)
            act.wait_ge(alibi_done, GRP)
            nc.scalar.activation(alibi_hi[:, :, :], alibi[:, :, :], ACT.Copy).then_inc(alibi_hi_done, 1)
            copy_out(zt_hi[0][:, :, :], zt_ps[0][:, :], zt_turned, 1, zt_hi_ready)
            fc_sums(range(0, 1))
            weight_high(0, k_in, k_w_hi)
            weight_high(2, v_in, v_w_hi)
            fc_sums(range(1, 3))
            norm_std(0, var1, std1, 1)
            act.wait_ge(std1, 2)
            nc.scalar.activation(table_junk[:, :], eps_sb[:, :], ACT.Exp)

            def first_part(dst, f, ps, done, ready):
                act.wait_ge(done, f + 1)
                nc.scalar.activation(dst[:, f, 0, :, 0:S], ps[f][:, :].rearrange("p (n s) -> p n s", s=S),
                                     ACT.Copy).then_inc(ready, 1)

            def spread(f, n, dst, src, ready, signal, between=None):
                act.wait_ge(ready, f + 1)
                for a in range(SPREAD_DVE, SPREAD_DVE + SPREAD_ACT):
                    if between and a == SPREAD_DVE + 1:
                        between()
                    last = nc.scalar.activation(dst[:, f, :, n, a, :], src[:, f, :, n, :], ACT.Copy,
                                                scale=mask[:, a:a + 1])
                last.then_inc(signal, 1)

            def mlp_sums(o):
                act.wait_ge(mlp_in, 16)
                if o > 0:
                    act.wait_ge(mlp_summed, o)
                nc.scalar.activation(mlp_junk, mlp_sb[:, o, :], ACT.Abs,
                                     accum_out=mlp_sum[:, o:o + 1]).then_inc(mlp_summed, 1)

            def exponentials(f):
                act.wait_ge(shift_ready, f + 1)
                nc.scalar.activation(prob[:, f, :, :], shifted[:, f, :, :], ACT.Exp,
                                     scale=float(D) ** -0.5).then_inc(prob_ready, 1)

            first_part(q_part, 0, q_ps, q_done, q_first)
            fc_sums(range(3, 5))
            copy_out(zt_hi[1][:, :, :], zt_ps[1][:, :], zt_turned, 2, zt_hi_ready)
            first_part(k_part, 0, k_ps, k_done, k_first)
            fc_sums(range(5, KH))
            spread(0, ALL, q_spread, q_part, q_ready, q_spread_act)
            first_part(q_part, 1, q_ps, q_done, q_first)
            first_part(k_part, 1, k_ps, k_done, k_first)
            spread(1, ALL, q_spread, q_part, q_ready, q_spread_act)
            first_part(v_part, 0, v_ps, v_done, v_first)
            first_part(v_part, 1, v_ps, v_done, v_first)
            exponentials(0)
            mlp_sums(0)
            first_part(p_part, 0, pt_ps, pt_turned, p_first)
            mlp_sums(1)
            spread(0, FIRST, p_spread, p_part, p_ready, p_spread_act)
            for i in range(2):
                copy_out(u_t[:, i * HT * 2:(i + 1) * HT * 2], ut_ps[i], ut_turned, i + 1, ut_ready)
            exponentials(1)
            spread(0, SECOND, p_spread, p_part, p_ready, p_spread_act,
                   between=lambda: first_part(p_part, 1, pt_ps, pt_turned, p_first))
            spread(1, FIRST, p_spread, p_part, p_ready, p_spread_act)
            spread(1, SECOND, p_spread, p_part, p_ready, p_spread_act)
            copy_out(yt_hi[0][:, :, :], yt_ps[0][:, :], yt_turned, 1, yt_hi_ready)
            for k in range(KE):
                copy_out(fc_t[:, k, :], fct_ps[k], fct_turned, k + 1, fct_ready)
            act.wait_ge(prob_ready, 2)
            nc.scalar.activation(table_junk[:, :], eps_sb[:, :], ACT.Sqrt)
            copy_out(yt_hi[1][:, :, :], yt_ps[1][:, :], yt_turned, 2, yt_hi_ready)
            norm_std(1, var2, std2, 0)
            for i in range(2):
                copy_out(mlp_t[:, 4 * i:4 * i + 4, :], mlpt_ps[i], mlpt_turned, i + 1, mlpt_ready)
            copy_out(z2t_hi[0][:, :, :], z2t_ps[0][:, :], z2t_turned, 1, z2t_hi_ready)

            def low_a_copy(f):
                copy_out(low_a[:, f, :], low_ps[f][0:2 * RANK, 0:HT], low_a_done, f + 1, low_a_ready)

            def low_high(f):
                act.wait_ge(low_c_done, f + 1)
                nc.scalar.activation(low_t[:, f, :], low_ps[f][0:4 * RANK, HT:2 * HT],
                                     ACT.Copy).then_inc(low_hi_ready, 1)

            low_a_copy(0)
            norm_std(1, var2, std2, 1)
            low_high(0)

            def squares(n):
                f, j = divmod(n, PAIRS)
                if n >= RING:
                    act.wait_ge(sq_ready, n - RING + 1)
                act.wait_ge(fc_done, n + 1)
                for a in range(2):
                    m = 2 * j + a
                    nc.scalar.activation(relu[:, n % RING, a, :], FCB[n % len(FCB)][:, a * HT:(a + 1) * HT],
                                         ACT.Relu, scale=fc_scale[:, 0, m:m + 1]).then_inc(relu_ready, 1)
                if n >= RING:
                    act.wait_ge(mlp_step, n - RING + 1)
                act.wait_ge(relu_ready, 2 * n + 2)
                nc.scalar.activation(sq_hi[:, n % RING, :, :], relu[:, n % RING, :, :],
                                     ACT.Square).then_inc(sq_hi_ready, 1)

            squares(0)
            copy_out(z2t_hi[1][:, :, :], z2t_ps[1][:, :], z2t_turned, 2, z2t_hi_ready)
            copy_out(h2_t[:, 0, :, :], h2t_ps[0][:, :], h2t_turned, 1, h2t_ready)
            squares(1)
            squares(2)
            copy_out(h2_t[:, 1, :, :], h2t_ps[1][:, :], h2t_turned, 2, h2t_ready)
            low_high(1)
            for n in range(3, HALVES * PAIRS):
                squares(n)

        @block.vector
        def _(dve):
            dve.memset(warm[:, :], 0.0).then_inc(warm_set, 1)
            dve.memset(eps_sb[:, :], EPS).then_inc(eps_set, 1)
            def scales(sums, scale, n, length, summed, scaled):
                dve.wait_ge(summed, n)
                dve.tensor_scalar(scale[:, 0, :], sums[:, :], 1.0 / length, EPS, ALU.mult,
                                  ALU.max).then_inc(scaled, 1)
                dve.wait_ge(scaled, 1)
                dve.tensor_scalar(scale[:, 1, :], scale[:, 0, :], 0.5, None, ALU.mult).then_inc(scaled, 1)
                dve.tensor_scalar(scale[:, 2, :], scale[:, 0, :], -0.5, None, ALU.mult).then_inc(scaled, 1)

            def ternary(w, scale, tern, m, cmp, ready):
                dve.wait_ge(cmp, m + 1)
                dve.scalar_tensor_tensor(tern[:, m, :], w[:, m, :], scale[:, 1, m:m + 1], tern[:, m, :],
                                         ALU.is_gt, ALU.subtract).then_inc(ready, 1)

            dve.wait_ge(bias_set, 2)
            dve.tensor_tensor(bias_parts[32:33, :], bias_sb[32:33, :],
                              bias_parts[32:33, :].bitcast(F32), ALU.subtract).then_inc(bias_set, 1)

            def score_bias():
                dve.wait_ge(const_in, 16)
                dve.wait_ge(slope_in, 16)
                for g in range(GRP):
                    dve.scalar_tensor_tensor(alibi[:, g, :], rel, slope_sb[:, g:g + 1], neg, ALU.mult,
                                             ALU.add).then_inc(alibi_done, 1)

            def score_bias_low():
                dve.tensor_copy(ident_r[:, :], ident).then_inc(identr_done, 1)
                dve.tensor_copy(ident_bf[:, :], ident).then_inc(identbf_done, 1)
                dve.wait_ge(alibi_hi_done, 1)
                dve.tensor_tensor(alibi_lo[:, :, :], alibi[:, :, :], alibi_hi[:, :, :].bitcast(F32),
                                  ALU.subtract).then_inc(alibi_ready, 1)

            def low_rank_factors():
                dve.wait_ge(rows_in, 32)
                dve.wait_ge(small_in, 16 * SMALL_LOADS)
                dve.reciprocal(fc_scale[:, 3, :], fc_scale[:, 0, :]).then_inc(u_step, 1)
                dve.wait_ge(u_step, 1)
                recip = fc_scale[:, 3, :].rearrange("p (m o) -> p m o", o=1).broadcast_to([P, KH, RANK])
                dve.scalar_tensor_tensor(u_scaled[:, :, :], u_sb[:, :, :], rows_sb[:, R_GATE:R_GATE + 1],
                                         recip, ALU.mult, ALU.mult).then_inc(u_step, 1)
                dve.wait_ge(u_step, 2)
                dve.tensor_copy(u_parts[:, :, 0, :], u_scaled[:, :, :]).then_inc(u_step, 1)
                dve.tensor_copy(u_parts[:, :, 2, :], u_scaled[:, :, :]).then_inc(u_step, 1)
                dve.wait_ge(u_step, 4)
                for part in (1, 3):
                    dve.tensor_tensor(u_parts[:, :, part, :], u_scaled[:, :, :],
                                      u_parts[:, :, part - 1, :].bitcast(F32), ALU.subtract).then_inc(u_step, 1)

            def stats(b, which, hidden_state, src, other, src_done, count, h_sem, bn_sem, var_sem):
                dve.wait_ge(src_done, count)
                dve.tensor_tensor(hidden_state[:, b, :], src, other, ALU.add).then_inc(h_sem, 1)
                dve.wait_ge(h_sem, b + 1)
                dve.bn_stats(bn6[:, which, b, :], hidden_state[:, b, :]).then_inc(bn_sem, 1)
                dve.wait_ge(bn_sem, b + 1)
                dve.bn_aggr(mv[:, which, b, :], bn6[:, which, b, :]).then_inc(var_sem, 1)

            def normalise(f, which, hidden_state, std_sem, rstd_sem, z_sem):
                dve.wait_ge(std_sem, f + 1)
                dve.reciprocal(rstd[:, which, f * BH:(f + 1) * BH],
                               std[:, which, f * BH:(f + 1) * BH]).then_inc(rstd_sem, 1)
                dve.wait_ge(rstd_sem, f + 1)
                for b in range(f * BH, (f + 1) * BH):
                    dve.tensor_scalar(z[:, b, :], hidden_state[:, b, :], mv[:, which, b, 0:1],
                                      rstd[:, which, b:b + 1], ALU.subtract, ALU.mult).then_inc(z_sem, 1)

            def low_part(dst, src, hi, count, hi_ready, signal):
                dve.wait_ge(hi_ready, count)
                dve.tensor_tensor(dst, src, hi.bitcast(F32), ALU.subtract).then_inc(signal, 1)

            def stats1(b):
                stats(b, 0, h1, tok_ps[b], posb[:, :], tok_done, b + 1, h1_ready, bn1, var1)

            def stats2(b):
                dve.wait_ge(residual_ready, b // BH + 1)
                stats(b, 1, h2, o_ps[b], h1[:, b, :], o_done, b + 1, h2_ready, bn2, var2)

            def zt_low(f):
                low_part(zt_lo[f][:, :, :], zt_ps[f][:, :].rearrange("p (k t) -> p k t", k=KE),
                         zt_hi[f][:, :, :], f + 1, zt_hi_ready, zt_lo_ready)

            def yt_low(f):
                low_part(yt_lo[f][:, :, :], yt_ps[f][:, :].rearrange("p (g t) -> p g t", g=GRP),
                         yt_hi[f][:, :, :], f + 1, yt_hi_ready, yt_lo_ready)

            def z2t_low(f):
                low_part(z2t_lo[f][:, :, :], z2t_ps[f][:, :].rearrange("p (k t) -> p k t", k=KE),
                         z2t_hi[f][:, :, :], f + 1, z2t_hi_ready, z2t_lo_ready)

            def spread(f, n, dst, src, ready, signal):
                dve.wait_ge(ready, f + 1)
                for a in range(SPREAD_DVE):
                    last = dve.tensor_scalar(dst[:, f, :, n, a, :], src[:, f, :, n, :], mask[:, a:a + 1],
                                             None, ALU.mult)
                last.then_inc(signal, 1)

            def left_over(f, ps, part, left, first, signal):
                dve.wait_ge(first, f + 1)
                dve.tensor_tensor(left[:, f, :, :], ps[f][:, :].rearrange("p (n s) -> p n s", s=S),
                                  part[:, f, 0, :, 0:S], ALU.subtract).then_inc(signal, 1)

            def later_parts(f, part, left, left_ready, second, ready):
                dve.wait_ge(left_ready, f + 1)
                dve.tensor_copy(part[:, f, 1, :, :], left[:, f, :, :]).then_inc(second, 1)
                dve.wait_ge(second, f + 1)
                dve.tensor_tensor(part[:, f, 2, :, :], left[:, f, :, :], part[:, f, 1, :, :],
                                  ALU.subtract).then_inc(ready, 1)

            def per_key(t, f):
                return t[:, f, :].rearrange("p (n o) -> p n o", o=1).broadcast_to([P, GRP * IPH, S])

            def softmax_shift(f):
                dve.wait_ge(s_done, GRP * (f + 1))
                rows_ = s_ps[f][:, :].rearrange("p (n s) -> p n s", s=S)
                dve.tensor_reduce(smax[:, f, :], rows_, AX.X, ALU.max).then_inc(max_ready, 1)
                dve.wait_ge(max_ready, f + 1)
                dve.tensor_tensor(shifted[:, f, :, :], rows_, per_key(smax, f),
                                  ALU.subtract).then_inc(shift_ready, 1)

            def attention_rows(f, b):
                dve.wait_ge(y_done, BH * f + b + 1)
                y = y_ps[f][b][:, 0:H * (D + 1)].rearrange("p (h d) -> p h d", d=D + 1)
                dve.reciprocal(srec[:, f, b, :], y[:, :, D]).then_inc(norm_ready, 1)
                dve.wait_ge(norm_ready, BH * f + b + 1)
                scale = srec[:, f, b, :].rearrange("p (h o) -> p h o", o=1).broadcast_to([P, H, D])
                dve.tensor_tensor(y_tok[:, f, b, :].rearrange("p (h d) -> p h d", d=D), y[:, :, 0:D], scale,
                                  ALU.mult).then_inc(y_ready, 1)

            def query_parts(f):
                left_over(f, q_ps, q_part, rest, q_first, q_rest)
                later_parts(f, q_part, rest, q_rest, q_second, q_ready)
                left_over(f, k_ps, k_part, rest_k, k_first, k_rest)

            def prob_parts(f):
                left_over(f, pt_ps, p_part, rest, p_first, p_rest)
                later_parts(f, p_part, rest, p_rest, p_second, p_ready)

            dve.wait_ge(posb_done, 1)
            stats1(0)
            stats1(1)
            score_bias()
            normalise(0, 0, h1, std1, rstd1, z1_ready)
            stats1(2)
            score_bias_low()
            zt_low(0)
            stats1(3)
            normalise(1, 0, h1, std1, rstd1, z1_ready)
            left_over(0, q_ps, q_part, rest, q_first, q_rest)
            zt_low(1)
            later_parts(0, q_part, rest, q_rest, q_second, q_ready)
            left_over(0, k_ps, k_part, rest_k, k_first, k_rest)
            scales(fc_sum, fc_scale, KH, E, fc_summed, fc_scaled)
            spread(0, ALL, q_spread, q_part, q_ready, q_spread_dve)
            left_over(1, q_ps, q_part, rest, q_first, q_rest)
            later_parts(1, q_part, rest, q_rest, q_second, q_ready)
            left_over(1, k_ps, k_part, rest_k, k_first, k_rest)
            spread(1, ALL, q_spread, q_part, q_ready, q_spread_dve)
            def fc_ternaries(tiles):
                for m in tiles:
                    ternary(fc_sb, fc_scale, fc_tern, m, fc_cmp, fc_ternary)

            fc_ternaries(range(0, 2))
            softmax_shift(0)
            left_over(0, v_ps, v_part, rest_v, v_first, v_rest)
            left_over(1, v_ps, v_part, rest_v, v_first, v_rest)
            low_rank_factors()
            prob_parts(0)
            spread(0, FIRST, p_spread, p_part, p_ready, p_spread_dve)
            softmax_shift(1)
            scales(mlp_sum, mlp_scale, KE, HID, mlp_summed, mlp_scaled)
            spread(0, SECOND, p_spread, p_part, p_ready, p_spread_dve)
            prob_parts(1)
            spread(1, FIRST, p_spread, p_part, p_ready, p_spread_dve)
            attention_rows(0, 0)
            attention_rows(0, 1)
            spread(1, SECOND, p_spread, p_part, p_ready, p_spread_dve)
            fc_ternaries(range(2, KH))
            yt_low(0)
            ternary(mlp_sb, mlp_scale, mlp_tern, 0, mlp_cmp, mlp_ternary)
            attention_rows(1, 0)
            attention_rows(1, 1)
            ternary(mlp_sb, mlp_scale, mlp_tern, 1, mlp_cmp, mlp_ternary)
            stats2(0)
            stats2(1)
            yt_low(1)
            normalise(0, 1, h2, std2, rstd2, z2_ready)
            stats2(2)
            z2t_low(0)
            def low_a_copy(f):
                dve.wait_ge(low_a_done, f + 1)
                dve.tensor_copy(low_a[:, f, :], low_ps[f][0:2 * RANK, 0:HT]).then_inc(low_a_ready, 1)

            def low_low(f):
                dve.wait_ge(low_hi_ready, f + 1)
                dve.tensor_tensor(low_t[2 * RANK:4 * RANK, f, :], low_ps[f][2 * RANK:4 * RANK, HT:2 * HT],
                                  low_t[2 * RANK:4 * RANK, f, :].bitcast(F32),
                                  ALU.subtract).then_inc(low_ready, 1)

            def result(f, m):
                if f == 1 and m == 0:
                    dve.wait_ge(mlp_tile, 2)
                else:
                    dve.wait_ge(mlp_step, PAIRS * (f + 1))
                dve.wait_ge(h2t_ready, f + 1)
                dve.scalar_tensor_tensor(out_sb[:, f, m, :], mlp_ps[f][m], mlp_scale[:, 0, m:m + 1],
                                         h2_t[:, f, m, :], ALU.mult, ALU.add).then_inc(out_ready, 1)

            def squares(n):
                r = n % RING
                dve.wait_ge(relu_ready, 2 * n + 2)
                if n >= RING:
                    dve.wait_ge(mlp_step, n - RING + 1)
                dve.tensor_tensor(sq[:, r, :, :], relu[:, r, :, :], relu[:, r, :, :],
                                  ALU.mult).then_inc(sq_ready, 1)
                dve.wait_ge(sq_ready, n + 1)
                low_part(sq_lo[:, r, :, :], sq[:, r, :, :], sq_hi[:, r, :, :], n + 1, sq_hi_ready,
                         sq_lo_ready)

            stats2(3)
            normalise(1, 1, h2, std2, rstd2, z2_ready)
            low_low(0)
            squares(0)
            z2t_low(1)
            squares(1)
            low_a_copy(1)
            squares(2)
            low_low(1)
            squares(3)
            for n in range(PAIRS, HALVES * PAIRS):
                squares(n)
            for f in range(HALVES):
                for m in range(KE):
                    result(f, m)

        @block.gpsimd
        def _(pool):
            def split(w, hi, lo, signal):
                pool.tensor_scalar(hi, w, 1.0, 1.0, ALU.mult, ALU.mult).then_inc(signal, 1)
                pool.wait_ge(signal, 1)
                pool.tensor_tensor(lo, w, hi.bitcast(F32), ALU.subtract).then_inc(signal, 1)

            pool.memset(bias_parts[:, :].bitcast(F32), 0.0).then_inc(bias_set, 1)
            pool.memset(ones_f[:, :], 1.0).then_inc(ones_set, 1)
            pool.wait_ge(ones_set, 1)
            pool.tensor_scalar(ones[:, :], ones_f[:, :], 1.0, 1.0, ALU.mult, ALU.mult).then_inc(ones_set, 1)
            for i in range(PARTS):
                pool.memset(v_part[:, :, i, :, D:VW], 1.0 if i == 0 else 0.0).then_inc(v_ones_set, 1)
            pool.wait_ge(rows_in, 32)
            pool.tensor_tensor(posb[:, :], pos_sb[:, :], rows_sb[:, R_TOKB:R_TOKB + E],
                               ALU.add).then_inc(posb_done, 1)
            for which, hi_ready, signal in ((1, q_w_hi, q_split), (0, k_w_hi, k_split),
                                            (2, v_w_hi, v_w_split)):
                c = which * E
                pool.wait_ge(hi_ready, 1)
                pool.tensor_tensor(kqv_lo[:, :, c:c + E], kqv_sb[:, :, c:c + E],
                                   kqv_hi[:, :, c:c + E].bitcast(F32), ALU.subtract).then_inc(signal, 1)
            def later_parts(f, part, left, left_ready, second, ready):
                pool.wait_ge(left_ready, f + 1)
                pool.tensor_scalar(part[:, f, 1, :, 0:S], left[:, f, :, :], 1.0, 1.0, ALU.mult,
                                   ALU.mult).then_inc(second, 1)
                pool.wait_ge(second, f + 1)
                pool.tensor_tensor(part[:, f, 2, :, 0:S], left[:, f, :, :], part[:, f, 1, :, 0:S],
                                   ALU.subtract).then_inc(ready, 1)

            def below(w, scale, dst, tiles, scaled, signal):
                pool.wait_ge(scaled, 3)
                for m in tiles:
                    pool.tensor_scalar(dst[:, m, :], w[:, m, :], scale[:, 2, m:m + 1], None,
                                       ALU.is_lt).then_inc(signal, 1)

            def spread(f, n, dst, src, ready, signal):
                pool.wait_ge(ready, f + 1)
                for a in range(SPREAD_DVE + SPREAD_ACT, 8):
                    last = pool.tensor_scalar(dst[:, f, :, n, a, :], src[:, f, :, n, :], mask[:, a:a + 1],
                                              1.0, ALU.mult, ALU.mult)
                last.then_inc(signal, 1)

            pool.wait_ge(proj_in, 16)
            split(proj_sb[:, :, :], proj_hi[:, :, :], proj_lo[:, :, :], proj_split)
            pool.wait_ge(proj_bias_in, 16)
            for f in range(HALVES):
                pool.wait_ge(z1_ready, BH * (f + 1))
                rows_ = h1[:, f * BH:(f + 1) * BH, :]
                pool.tensor_tensor(rows_, rows_,
                                   proj_bias_sb[:, :].rearrange("p (o e) -> p o e", o=1
                                                                ).broadcast_to([P, BH, E]),
                                   ALU.add).then_inc(residual_ready, 1)
            later_parts(0, k_part, rest_k, k_rest, k_second, k_ready)
            spread(0, ALL, q_spread, q_part, q_ready, q_spread_pool)
            below(fc_sb, fc_scale, fc_tern, range(0, 2), fc_scaled, fc_cmp)
            spread(1, ALL, q_spread, q_part, q_ready, q_spread_pool)
            later_parts(1, k_part, rest_k, k_rest, k_second, k_ready)
            later_parts(0, v_part, rest_v, v_rest, v_second, v_ready)
            below(fc_sb, fc_scale, fc_tern, range(2, 4), fc_scaled, fc_cmp)
            spread(0, FIRST, p_spread, p_part, p_ready, p_spread_pool)
            spread(0, SECOND, p_spread, p_part, p_ready, p_spread_pool)
            later_parts(1, v_part, rest_v, v_rest, v_second, v_ready)
            below(fc_sb, fc_scale, fc_tern, range(4, 6), fc_scaled, fc_cmp)
            spread(1, FIRST, p_spread, p_part, p_ready, p_spread_pool)
            spread(1, SECOND, p_spread, p_part, p_ready, p_spread_pool)
            below(fc_sb, fc_scale, fc_tern, range(6, KH), fc_scaled, fc_cmp)
            below(mlp_sb, mlp_scale, mlp_tern, range(KE), mlp_scaled, mlp_cmp)
            pool.wait_ge(small_in, 16 * SMALL_LOADS)
            split(v_sb[:, :, :], v_parts[:, :, 0, :], v_parts[:, :, 1, :], v_split)


def shape_constants():
    p = np.arange(P)
    key, query = np.arange(S)[None, :], (p % S)[:, None]
    c = np.zeros((P, C_END), np.float32)
    c[:, C_ID:C_ID + P] = np.eye(P)
    c[:, C_MASK:C_MASK + 8] = p[:, None] // 16 == np.arange(8)[None, :]
    c[:, C_REL:C_REL + S] = D ** 0.5 * np.where(key <= query, key - query, 0)
    c[:, C_NEG:C_NEG + S] = D ** 0.5 * np.where(key > query, NEG_INF, 0.0)
    return c


def kernel(x, L0_tok_W, L0_tok_b, L0_tok_pos_emb, L0_attn_W_kqv, L0_attn_b_kqv, L0_attn_W_proj,
           L0_attn_b_proj, L0_attn_slopes, L0_ffn_fast_b, L0_ffn_w_fc, L0_ffn_w_proj, L0_ffn_u,
           L0_ffn_v, L0_ffn_gate):
    import concourse.bacc as bacc
    from concourse.bass_utils import run_bass_kernel_spmd

    a = np.asarray
    patches = a(x).reshape(IMAGES, CH, SIDE, PATCH, SIDE, PATCH).transpose(1, 3, 5, 0, 2, 4)
    arrays = {
        "x_t": patches.reshape(FEAT, TOK),
        "wtok_t": a(L0_tok_W).T,
        "consts": shape_constants(),
        "rows": np.concatenate([a(L0_tok_b), a(L0_ffn_gate).reshape(1)]).reshape(1, R_END),
        "pos": np.tile(a(L0_tok_pos_emb), (IPB, 1)),
        "w_kqv": a(L0_attn_W_kqv),
        "bias_row": a(L0_attn_b_kqv).reshape(1, 3 * E),
        "proj_bias": a(L0_attn_b_proj).reshape(1, E),
        "slopes": np.repeat(a(L0_attn_slopes).reshape(GRP, HPG), S, axis=1).T,
        "w_proj": a(L0_attn_W_proj),
        "w_fc": a(L0_ffn_w_fc),
        "w_mlp": a(L0_ffn_w_proj),
        "u_nat": a(L0_ffn_u),
        "v_t": a(L0_ffn_v).T,
        "fb_t": a(L0_ffn_fast_b).T,
    }
    arrays = {n: np.ascontiguousarray(t) for n, t in arrays.items()}
    nc = bacc.Bacc("TRN2", target_bir_lowering=False, num_devices=1)
    args = {n: nc.dram_tensor(n, t.shape, mybir.dt.from_np(t.dtype), kind="ExternalInput").ap()
            for n, t in arrays.items()}
    out_t = nc.dram_tensor("out_t", (E, TOK), F32, kind="ExternalOutput").ap()
    build_program(nc, out_t=out_t, **args)
    got = run_bass_kernel_spmd(nc, [arrays], core_ids=[0])
    return a(got.results[0]["out_t"]).T.reshape(IMAGES, S, E)
```
